# Optimizing a Trainium2 kernel written in Bass

```python
import numpy as np
import jax
import jax.numpy as jnp

def _softmax(x, axis=-1):
    return jax.nn.softmax(x, axis=axis)

def _gelu(x):
    return jax.nn.gelu(x, approximate=True)

def _silu(x):
    return jax.nn.silu(x)

def _sigmoid(x):
    return jax.nn.sigmoid(x)

def _layernorm(x, axis=-1, eps=1e-05):
    m = jnp.mean(x, axis=axis, keepdims=True)
    v = jnp.var(x, axis=axis, keepdims=True)
    return (x - m) / jnp.sqrt(v + eps)

def _scatter_add(tgt, idx, src, axis=0):
    return tgt.at[idx].add(src)

def _segment_sum(src, seg, n):
    return jax.ops.segment_sum(src, seg, n)
kernel_name = 'mk_flamingo_gated_d2_seqx_r8_0221ed'

def setup_inputs(seed: int=0):
    np.random.seed(seed)
    _w = jnp.asarray

    def _rec_inputs():
        import jax
        import jax.numpy as jnp
        _rk = jax.random.key(seed)
        x = 0.5 + 0.2887 * jax.random.normal(jax.random.fold_in(_rk, 1), (4, 256, 256), jnp.float32)
        _lenS = 256 - jax.random.randint(jax.random.fold_in(_rk, 7), (4,), 0, max(1, 256 // 4) + 1, jnp.int32)
        _lenS2 = 256 - jax.random.randint(jax.random.fold_in(_rk, 8), (4,), 0, max(1, 256 // 4) + 1, jnp.int32)
        _ctx_512P = jax.random.normal(jax.random.fold_in(_rk, 11), (4, 16, 64), jnp.float32)
        _ctx_512c = jax.random.dirichlet(jax.random.fold_in(_rk, 511), 0.3 * jnp.ones((16,), jnp.float32), (4, 256))
        _ctx_512t = jnp.einsum('bsk,bkd->bsd', _ctx_512c, _ctx_512P)
        _ctx_512t = _ctx_512t * jax.lax.rsqrt(jnp.mean(jnp.square(_ctx_512t)) + 1e-12) * 0.953939
        ctx_512 = -0.000392918 + 0.999932 * (_ctx_512t + 0.3 * jax.random.normal(jax.random.fold_in(_rk, 611), (4, 256, 64), jnp.float32))
        _g = jax.random.normal(jax.random.fold_in(_rk, 9001), (2, 2), jnp.float32)
        _g = jnp.sign(_g) * jnp.maximum(jnp.abs(_g), 1.0) + (_g == 0) * 1.0
        g_xattn = _g[0]
        g_ffn = _g[1]
        return (x, ctx_512, g_xattn, g_ffn)
    x, ctx_512, g_xattn, g_ffn = _rec_inputs()

    def _L0_xattn_setup():
        import jax, jax.numpy as jnp
        import numpy as np
        B, N, D = (16, 256, 64)
        H = 4
        TOP_K_RATIO = 0.3
        key = jax.random.key(seed)
        k1, k2, k3, k4 = jax.random.split(key, 4)
        h = jax.random.normal(k1, (B, N, D), dtype=jnp.float32)
        adj_raw = jax.random.uniform(k2, (B, N, N), dtype=jnp.float32)
        lim = 1.0 / np.sqrt(D)
        Wq = jax.random.uniform(k3, (D, D), minval=-lim, maxval=lim, dtype=jnp.float32)
        Wk = jax.random.uniform(k4, (D, D), minval=-lim, maxval=lim, dtype=jnp.float32)
        gamma_raw = jnp.float32(-0.85)
        return {'h': h, 'adj_raw': adj_raw, 'Wq': Wq, 'Wk': Wk, 'gamma_raw': gamma_raw}
    _L0_xattn_all = _L0_xattn_setup()
    _L0_xattn_in = {k: v for k, v in _L0_xattn_all.items() if k in ('Wq', 'Wk', 'gamma_raw')}
    del _L0_xattn_all

    def _L0_ffn_setup():
        import jax, jax.numpy as jnp
        import numpy as np
        NUM_EXPERTS = 64
        TOP_K = 8
        HIDDEN = 256
        INTER = 128
        key = jax.random.key(seed)
        k1, k2, k3, k4 = jax.random.split(key, 4)
        scale = 1.0 / np.sqrt(HIDDEN)
        hidden_states = jax.random.normal(k1, (4, 256, HIDDEN), dtype=jnp.float32)
        gate_w = jax.random.normal(k2, (NUM_EXPERTS, HIDDEN), dtype=jnp.float32) * scale
        w13 = jax.random.normal(k3, (NUM_EXPERTS, 2 * INTER, HIDDEN), dtype=jnp.float32) * scale
        w2 = jax.random.normal(k4, (NUM_EXPERTS, HIDDEN, INTER), dtype=jnp.float32) * (1.0 / np.sqrt(INTER))
        return {'hidden_states': hidden_states, 'gate_w': gate_w, 'w13': w13, 'w2': w2}
    _L0_ffn_all = _L0_ffn_setup()
    _L0_ffn_in = {k: v for k, v in _L0_ffn_all.items() if k in ('gate_w', 'w13', 'w2')}
    del _L0_ffn_all

    def _L1_xattn_setup():
        import jax, jax.numpy as jnp
        import numpy as np
        B, S, H, NH, L = (2, 256, 256, 16, 64)
        HD = H // NH
        key = jax.random.key(seed)
        k1, k2, k3, k4, k5 = jax.random.split(key, 5)
        scale = 0.02
        return {'q': jax.random.normal(k1, (B, S, H), dtype=jnp.float32), 'latent_kv': jax.random.normal(k2, (B, S, L), dtype=jnp.float32), 'Wq': jax.random.normal(k3, (H, H), dtype=jnp.float32) * scale, 'Wkv_expand': jax.random.normal(k4, (2 * H, L), dtype=jnp.float32) * scale, 'Wout': jax.random.normal(k5, (H, H), dtype=jnp.float32) * scale}
    _L1_xattn_all = _L1_xattn_setup()
    _L1_xattn_in = {k: v for k, v in _L1_xattn_all.items() if k in ('Wq', 'Wkv_expand', 'Wout')}
    del _L1_xattn_all

    def _L1_ffn_setup():
        import jax, jax.numpy as jnp
        import numpy as np
        N_EXPERTS = 8
        TOP_K = 2
        C = 256
        H = 128
        HS = 256
        B, T = (1, 64)
        SCALE = 0.02
        key = jax.random.key(seed)
        ks = jax.random.split(key, 10)
        x = jax.random.normal(ks[0], (B, T, C), dtype=jnp.float32)
        gate_w = jax.random.normal(ks[1], (N_EXPERTS, C), dtype=jnp.float32) * SCALE
        w_gate = jax.random.normal(ks[2], (N_EXPERTS, H, C), dtype=jnp.float32) * SCALE
        w_up = jax.random.normal(ks[3], (N_EXPERTS, H, C), dtype=jnp.float32) * SCALE
        w_down = jax.random.normal(ks[4], (N_EXPERTS, C, H), dtype=jnp.float32) * SCALE
        sh_gate = jax.random.normal(ks[5], (HS, C), dtype=jnp.float32) * SCALE
        sh_up = jax.random.normal(ks[6], (HS, C), dtype=jnp.float32) * SCALE
        sh_down = jax.random.normal(ks[7], (C, HS), dtype=jnp.float32) * SCALE
        se_gate_w = jax.random.normal(ks[8], (1, C), dtype=jnp.float32) * SCALE
        return {'x': x, 'gate_w': gate_w, 'w_gate': w_gate, 'w_up': w_up, 'w_down': w_down, 'sh_gate': sh_gate, 'sh_up': sh_up, 'sh_down': sh_down, 'se_gate_w': se_gate_w}
    _L1_ffn_all = _L1_ffn_setup()
    _L1_ffn_in = {k: v for k, v in _L1_ffn_all.items() if k in ('gate_w', 'w_gate', 'w_up', 'w_down', 'sh_gate', 'sh_up', 'sh_down', 'se_gate_w')}
    del _L1_ffn_all
    return {'x': x, 'ctx_512': ctx_512, 'g_xattn': g_xattn, 'g_ffn': g_ffn, 'L0_xattn_Wq': _L0_xattn_in['Wq'], 'L0_xattn_Wk': _L0_xattn_in['Wk'], 'L0_xattn_gamma_raw': _L0_xattn_in['gamma_raw'], 'L0_ffn_gate_w': _L0_ffn_in['gate_w'], 'L0_ffn_w13': _L0_ffn_in['w13'], 'L0_ffn_w2': _L0_ffn_in['w2'], 'L1_xattn_Wq': _L1_xattn_in['Wq'], 'L1_xattn_Wkv_expand': _L1_xattn_in['Wkv_expand'], 'L1_xattn_Wout': _L1_xattn_in['Wout'], 'L1_ffn_gate_w': _L1_ffn_in['gate_w'], 'L1_ffn_w_gate': _L1_ffn_in['w_gate'], 'L1_ffn_w_up': _L1_ffn_in['w_up'], 'L1_ffn_w_down': _L1_ffn_in['w_down'], 'L1_ffn_sh_gate': _L1_ffn_in['sh_gate'], 'L1_ffn_sh_up': _L1_ffn_in['sh_up'], 'L1_ffn_sh_down': _L1_ffn_in['sh_down'], 'L1_ffn_se_gate_w': _L1_ffn_in['se_gate_w']}

def reference(x, ctx_512, g_xattn, g_ffn, L0_xattn_Wq, L0_xattn_Wk, L0_xattn_gamma_raw, L0_ffn_gate_w, L0_ffn_w13, L0_ffn_w2, L1_xattn_Wq, L1_xattn_Wkv_expand, L1_xattn_Wout, L1_ffn_gate_w, L1_ffn_w_gate, L1_ffn_w_up, L1_ffn_w_down, L1_ffn_sh_gate, L1_ffn_sh_up, L1_ffn_sh_down, L1_ffn_se_gate_w):
    import jax
    import jax.numpy as jnp

    def _L0_xattn_ref(h, adj_raw, Wq, Wk, gamma_raw):
        import jax, jax.numpy as jnp
        import numpy as np
        B, N, D = (16, 256, 64)
        H = 4
        TOP_K_RATIO = 0.3
        b, n, dm = h.shape
        d = dm // H
        Q = (h @ Wq.T).reshape(b, n, H, d).transpose(0, 2, 1, 3)
        K = (h @ Wk.T).reshape(b, n, H, d).transpose(0, 2, 1, 3)
        sim = jnp.einsum('bhnd,bhmd->bnm', Q, K) / (jnp.sqrt(jnp.float32(d)) * H)
        k = max(1, int(n * TOP_K_RATIO))
        topk_vals = jax.lax.top_k(sim, k)[0]
        threshold = topk_vals[:, :, -1:]
        sparse_mask = (sim >= threshold).astype(sim.dtype)
        A_learned = jax.nn.sigmoid(sim) * sparse_mask
        A_learned = (A_learned + jnp.swapaxes(A_learned, -1, -2)) * 0.5
        gamma = jax.nn.sigmoid(gamma_raw)
        return (1.0 - gamma) * adj_raw + gamma * A_learned

    def _L0_ffn_ref(hidden_states, gate_w, w13, w2):
        import jax, jax.numpy as jnp
        import numpy as np
        NUM_EXPERTS = 64
        TOP_K = 8
        HIDDEN = 256
        INTER = 128
        orig_shape = hidden_states.shape
        x = hidden_states.reshape(-1, HIDDEN)
        logits = jnp.einsum('th,eh->te', x, gate_w)
        probs = jax.nn.softmax(logits, axis=-1)
        topk_w, topk_idx = jax.lax.top_k(probs, TOP_K)
        combine = (jax.nn.one_hot(topk_idx, NUM_EXPERTS, dtype=x.dtype) * topk_w[..., None]).sum(axis=1)

        def step(acc, inp):
            w13_e, w2_e, c = inp
            g = x @ w13_e[:INTER].T
            u = x @ w13_e[INTER:].T
            h = jax.nn.silu(g) * u
            o = h @ w2_e.T
            return (acc + c[:, None] * o, None)
        out0 = jnp.zeros_like(x)
        out, _ = jax.lax.scan(step, out0, (w13, w2, combine.T))
        return out.reshape(orig_shape)

    def _L1_xattn_ref(q, latent_kv, Wq, Wkv_expand, Wout):
        import jax, jax.numpy as jnp
        import numpy as np
        B, S, H, NH, L = (2, 256, 256, 16, 64)
        HD = H // NH
        b, sq, _ = q.shape
        sk = latent_kv.shape[1]
        qp = q @ Wq.T
        kv = latent_kv @ Wkv_expand.T
        k, v = jnp.split(kv, 2, axis=-1)
        qh = qp.reshape(b, sq, NH, HD).transpose(0, 2, 1, 3)
        kh = k.reshape(b, sk, NH, HD).transpose(0, 2, 1, 3)
        vh = v.reshape(b, sk, NH, HD).transpose(0, 2, 1, 3)
        inv_sqrt_d = 1.0 / jnp.sqrt(jnp.float32(HD))
        scores = jnp.einsum('bhqd,bhkd->bhqk', qh, kh) * inv_sqrt_d
        causal = jnp.tril(jnp.ones((sq, sk), dtype=bool))
        scores = jnp.where(causal, scores, jnp.finfo(scores.dtype).min)
        attn = jax.nn.softmax(scores, axis=-1)
        out = jnp.einsum('bhqk,bhkd->bhqd', attn, vh)
        out = out.transpose(0, 2, 1, 3).reshape(b, sq, H)
        return out @ Wout.T

    def _L1_ffn_ref(x, gate_w, w_gate, w_up, w_down, sh_gate, sh_up, sh_down, se_gate_w):
        import jax, jax.numpy as jnp
        import numpy as np
        N_EXPERTS = 8
        TOP_K = 2
        C = 256
        H = 128
        HS = 256
        B, T = (1, 64)
        SCALE = 0.02
        Bb, Tt, Cc = x.shape
        xf = x.reshape(-1, Cc)
        scores = xf @ gate_w.T
        ew, ei = jax.lax.top_k(scores, TOP_K)
        ew = jax.nn.softmax(ew, axis=-1)
        x1 = jax.nn.silu(jnp.einsum('td,ehd->teh', xf, w_gate))
        x3 = jnp.einsum('td,ehd->teh', xf, w_up)
        expert_out = jnp.einsum('teh,edh->ted', x1 * x3, w_down)
        onehot = jax.nn.one_hot(ei, N_EXPERTS, dtype=ew.dtype)
        comb = jnp.einsum('ta,tae->te', ew, onehot)
        routed = jnp.einsum('te,ted->td', comb, expert_out)
        shared = jax.nn.silu(xf @ sh_gate.T) * (xf @ sh_up.T) @ sh_down.T
        sgate = jax.nn.sigmoid(xf @ se_gate_w.T)
        return (routed + sgate * shared).reshape(Bb, Tt, Cc)
    x = x + jnp.tanh(g_xattn[0]) * _L0_xattn_ref(ctx_512, _layernorm(x, axis=-1), L0_xattn_Wq, L0_xattn_Wk, L0_xattn_gamma_raw)
    x = x + jnp.tanh(g_ffn[0]) * _L0_ffn_ref(_layernorm(x, axis=-1), L0_ffn_gate_w, L0_ffn_w13, L0_ffn_w2)
    x = x + jnp.tanh(g_xattn[1]) * _L1_xattn_ref(_layernorm(x, axis=-1), ctx_512, L1_xattn_Wq, L1_xattn_Wkv_expand, L1_xattn_Wout)
    x = x + jnp.tanh(g_ffn[1]) * _L1_ffn_ref(_layernorm(x, axis=-1), L1_ffn_gate_w, L1_ffn_w_gate, L1_ffn_w_up, L1_ffn_w_down, L1_ffn_sh_gate, L1_ffn_sh_up, L1_ffn_sh_down, L1_ffn_se_gate_w)
    return x

_drawn_inputs = setup_inputs


def setup_inputs(seed=0):
    import zlib

    import numpy as np

    out = dict(_drawn_inputs(seed))
    spreads = {'g_ffn': (-1.0, 0.6)}
    factors = {'L1_xattn_Wq': 33.184,
     'L1_ffn_gate_w': 8.0,
     'L1_ffn_w_gate': 8.0,
     'L1_ffn_w_up': 7.964,
     'L1_ffn_w_down': 7.982,
     'L1_ffn_sh_gate': 7.965,
     'L1_ffn_sh_up': 7.919,
     'L1_ffn_sh_down': 7.895,
     'L1_ffn_se_gate_w': 8.0}
    for name, (base, spread) in spreads.items():
        noise = np.random.default_rng([zlib.crc32(name.encode()), seed]).standard_normal(out[name].shape)
        drawn = base * np.exp(spread * noise) if base else spread * noise
        out[name] = jnp.asarray(drawn.astype(out[name].dtype))
    for name, factor in factors.items():
        out[name] = (out[name] * factor).astype(out[name].dtype)
    return out
```

```python
from contextlib import ExitStack

import concourse.bass as bass
from concourse import mybir

F32 = mybir.dt.float32
BF16 = mybir.dt.bfloat16
I32 = mybir.dt.int32
ACT = mybir.ActivationFunctionType
ALU = mybir.AluOpType
AX = mybir.AxisListType
ds = bass.ds

P = 128
B, N, D = 4, 256, 256
DC = 64
T = B * N
TT = T // P
BT = N // P
KC = D // P
E0, TOP0 = 64, 8
I0 = 128
KTH = int(N * 0.3)
ROUNDS = (KTH + 7) // 8
NH, HD = 16, 16
HP = 32
HG, GH = NH * HP // P, P // HP
UNITS = NH // 2
E1 = 8
NF = E1 + 2
EPS = 1e-5
RSQRT_GUESS = float(0x5F3759DF)
NEWTON = 3
NORM_STEPS = 2 * BT + 2 + 3 * NEWTON
LOWEST = -3.0e38
SIM_SCALE = 1.0 / 16.0
HEAD_SCALE = HD ** -0.5


class Steps:

    def __init__(self, eng, sem):
        self.eng, self.sem, self.n = eng, sem, 0

    def done(self, ins):
        self.n += 1
        ins.then_inc(self.sem, 1)

    def wait(self, behind=0):
        self.eng.wait_ge(self.sem, self.n - behind)

    def end(self):
        self.wait()
        self.eng.sem_clear(self.sem)
        self.n = 0


def gated_block(nc, x, ctxT, raw, wqk0, gate0, wexp, wq1, wkv1, wo1, gate1, wgu1, wd1, cf, cb, out):
    with ExitStack() as ctx:
        def sb(name, shape, dt=F32):
            return ctx.enter_context(nc.sbuf_tensor(name, shape, dt))

        def sem(name):
            return ctx.enter_context(nc.semaphore(name))

        X = sb("X", [P, TT, D])
        CT = sb("CT", [DC, T])
        WQK0 = sb("WQK0", [DC, 2, P])
        GATE0 = sb("GATE0", [P, KC, E0])
        WQ1 = sb("WQ1", [P, KC, HG, P])
        WKV1 = sb("WKV1", [DC, 2, HG * P])
        WO1 = sb("WO1", [P, HG, D])
        GATE1 = sb("GATE1", [P, KC, E1 + 1])
        WGU1 = sb("WGU1", [P, NF, KC, 2, P])
        WD1 = sb("WD1", [P, NF, D])
        CF = sb("CF", [P, 2 * P + HG * P + 1])
        CB = sb("CB", [P, 5, P], BF16)
        ident, sel_den = CF[:, 0:P], CF[:, P:2 * P]
        sel_max = CF[0:NH, 2 * P:2 * P + HG * P].rearrange("p (g c) -> p g c", g=HG)
        k_one = CF[:, 2 * P + HG * P:2 * P + HG * P + 1]
        identb, mask_qk, mask_kq = CB[:, 0, :], CB[:, 1, :], CB[:, 2, :]
        RAW = sb("RAW", [P, 5])
        SC = sb("SC", [P, 8])
        X1 = sb("X1", [P, TT, D])
        XNT = sb("XNT", [P, KC, T])
        C0 = sb("C0", [P, TT, E0])
        MOE = sb("MOE", [P, TT, D])
        QK = sb("QK", [P, 2, N])
        SIM = sb("SIM", [P, BT, N])
        TH = sb("TH", [P, BT, N])
        WORK = sb("WORK", [P, BT, N])
        TOP = sb("TOP", [P, BT, 8])
        AM = sb("AM", [P, BT, N])
        BASE = sb("BASE", [P, BT, N])
        XW = sb("XW", [P, BT, D])
        XN = sb("XN", [P, BT, D])
        ST = sb("ST", [P, BT, 6])
        MV = sb("MV", [P, BT, 2])
        RS = sb("RS", [P, BT, 8])
        XB = sb("XB", [P, KC, N])
        LG = sb("LG", [P, BT, E0])
        LR = sb("LR", [P, BT, E0])
        EX = sb("EX", [P, BT, E0])
        L8 = sb("L8", [P, BT, 8])
        SM = sb("SM", [P, BT, 4])
        WE = sb("WE", [P, 2, 3 * D])
        SG = sb("SG", [P, 2, 512])
        HH = sb("HH", [P, 2, 512])
        CTB = sb("CTB", [DC, N])
        X2 = sb("X2", [P, BT, D])
        QT = sb("QT", [P, HG, N])
        KT = sb("KT", [P, HG, N])
        VA = sb("VA", [P, BT, NH, HP])
        NM = sb("NM", [P, BT, NH])
        MT = sb("MT", [NH, N])
        QM = sb("QM", [P, HG, N])
        PP = sb("PP", [P, 3, 2, N + P])
        OS = sb("OS", [P, HG, N])
        RD = sb("RD", [P, HG, N])
        ON = sb("ON", [P, HG, N])
        X3 = sb("X3", [P, BT, D])
        G14 = sb("G14", [P, BT, 16])
        G14R = sb("G14R", [P, BT, 16])
        TP = sb("TP", [P, BT, 8])
        T8 = sb("T8", [P, BT, 8])
        EG = sb("EG", [P, BT, 16])
        CM = sb("CM", [P, BT, E1 + 1])
        GS = sb("GS", [P, BT, 8])
        SG1 = sb("SG1", [P, 2, N])
        H1 = sb("H1", [P, 2, N])
        FA = sb("FA", [P, BT, D])
        OUT = sb("OUT", [P, BT, D])

        PS = ctx.enter_context(nc.psum_tensor("PS", [P, 8, 512], F32))

        def bank(i, **dims):
            shape = PS[:, i, :]
            return shape

        psQK = PS[:, 0, :].rearrange("p (a n) -> p a n", a=2)
        psS = PS[:, 1, :].rearrange("p (a n) -> p a n", a=2)
        psT = PS[:, 2, :].rearrange("p (a n) -> p a n", a=2)
        psX = PS[:, 3, :].rearrange("p (a n) -> p a n", a=2)
        psL = PS[:, 4, 0:BT * E0].rearrange("p (a n) -> p a n", a=BT)
        ps1 = PS[:, :, :].rearrange("p (s h) c -> p s h c", s=2)
        ps2 = PS[:, 0:6, :].rearrange("p (s h) c -> p s h c", s=3)
        psO = PS[:, 6:8, :].rearrange("p b (g n) -> p (b g) n", g=2)
        psQ = PS[:, 4:6, :].rearrange("p b (g n) -> p (b g) n", g=2)
        psK = PS[:, 6:8, :].rearrange("p b (g n) -> p (b g) n", g=2)
        psV = PS[:, 0:2, :].rearrange("p t (h c) -> p t h c", h=NH)
        psX3 = PS[:, 3, :].rearrange("p (a n) -> p a n", a=2)
        psM = PS[0:NH, 0, 0:N]
        psA = PS[:, 6:8, :].rearrange("p b (g n) -> p (b g) n", g=2)
        psD = PS[:, 0:2, :].rearrange("p b (g n) -> p (b g) n", g=2)
        psY = PS[:, 2, :].rearrange("p (a n) -> p a n", a=2)
        psG = PS[:, 2, 0:BT * (E1 + 1)].rearrange("p (a n) -> p a n", a=BT)
        psGU = PS[:, 4:6, :].rearrange("p s (a n) -> p s a n", a=2)
        psW = PS[:, 6:8, :].rearrange("p s (a n) -> p s a n", a=2)

        names = """loaded_ctx loaded_x loaded_raw loaded_gate0 loaded_l1 tanh_done scalars_done
            projected qk_copied scores_done sim_copied th_ready masked flipped xn_ready xn_flipped
            xnt_copied logits_done max_ready exp_done dve_scalar dve_mix act_mix x1_kept
            gu_done silu_done h_done o_done o_used
            e_ctx e_xn e_flip e_xt e_qkv e_qkv_copied e_s1 e_max e_flipmax e_mt e_sel
            e_qm e_s2 e_exp e_av e_os e_den e_on e_y e_xn3 e_flip3 e_xt3 e_gate e_gmax e_gexp
            e_gu e_silu e_h e_down e_acc e_out dve_l1 pool_set stored""".split()
        S = {n: sem(n) for n in names}
        w_loaded = [sem(f"w_loaded{i}") for i in range(2)]

        block = ctx.enter_context(nc.Block())

        @block.sync
        def _(sp):
            sp.dma_start(CT[:, :], ctxT).then_inc(S["loaded_ctx"], 16)
            sp.dma_start(WQK0[:, :, :], wqk0).then_inc(S["loaded_ctx"], 16)
            sp.dma_start(CF[:, :], cf).then_inc(S["loaded_ctx"], 16)
            sp.dma_start(X[:, :, :], x.rearrange("(t p) d -> p t d", p=P)).then_inc(S["loaded_x"], 16)
            sp.dma_start(RAW[:, :], raw.to_broadcast([P, 5])).then_inc(S["loaded_raw"], 16)
            sp.dma_start(GATE0[:, :, :], gate0).then_inc(S["loaded_gate0"], 16)
            for dst, src in ((WQ1[:, :, :, :], wq1), (WKV1[:, :, :], wkv1), (WO1[:, :, :], wo1),
                             (GATE1[:, :, :], gate1), (WGU1[:, :, :, :, :], wgu1), (WD1[:, :, :], wd1),
                             (CB[:, :, :], cb)):
                sp.dma_start(dst, src).then_inc(S["loaded_l1"], 16)
            for s in range(2):
                sp.dma_start(WE[:, s, :], wexp[s * P:(s + 1) * P, :]).then_inc(w_loaded[s], 16)
            with sp.Fori(1, E0 // 2) as i:
                for s in range(2):
                    sp.wait_ge(S["o_done"], (i * 2 + s - 1) * TT)
                    sp.dma_start(WE[:, s, :], wexp[ds(i * (2 * P) + s * P, P), :]).then_inc(w_loaded[s], 16)
            with sp.Fori(0, B) as b:
                sp.wait_ge(S["e_out"], b + 1)
                sp.dma_start(out[ds(b * N, N), :].rearrange("(t p) d -> p t d", p=P), OUT[:, :, :]).then_inc(S["stored"], 16)
            sp.wait_ge(S["stored"], 16 * B)

        @block.gpsimd
        def _(pool):
            nc.gpsimd.memset(VA[:, :, :, :], 0.0).then_inc(S["pool_set"], 1)
            pool.wait_ge(S["pool_set"], 1)
            nc.gpsimd.memset(VA[:, :, :, HD:HD + 1], 1.0).then_inc(S["pool_set"], 1)
            nc.gpsimd.memset(MOE[:, :, :], 0.0).then_inc(S["pool_set"], 1)
            nc.gpsimd.memset(G14[:, :, :], 1.0e30).then_inc(S["pool_set"], 1)
            nc.gpsimd.memset(TP[:, :, :], 1.0e30).then_inc(S["pool_set"], 1)
            pool.wait_ge(S["loaded_ctx"], 48)
            with pool.Fori(0, B) as b:
                pool.wait_ge(S["e_qkv"], b)
                nc.gpsimd.tensor_copy(CTB[:, :], CT[:, ds(b * N, N)]).then_inc(S["e_ctx"], 1)

        @block.tensor
        def _(pe):
            mm = nc.tensor.matmul
            pe.wait_ge(S["loaded_ctx"], 48)
            with pe.Fori(0, B) as b:
                pe.wait_ge(S["qk_copied"], b)
                for a in range(2):
                    last = mm(psQK[:, a, :], WQK0[:, a, :], CT[:, ds(b * N, N)], start=True, stop=True)
                last.then_inc(S["projected"], 1)
                pe.wait_ge(S["qk_copied"], b + 1)
                pe.wait_ge(S["sim_copied"], b)
                for t in range(BT):
                    last = mm(psS[:, t, :], QK[:, 0, t * P:(t + 1) * P], QK[:, 1, :], start=True, stop=True)
                last.then_inc(S["scores_done"], 1)
                pe.wait_ge(S["masked"], b + 1)
                for t in range(BT):
                    for c in range(BT):
                        last = nc.tensor.transpose(psT[:, t, c * P:(c + 1) * P], AM[:, c, t * P:(t + 1) * P], ident)
                last.then_inc(S["flipped"], 1)
                pe.wait_ge(S["xn_ready"], b + 1)
                for k in range(KC):
                    for t in range(BT):
                        last = nc.tensor.transpose(psX[:, k, t * P:(t + 1) * P], XN[:, t, k * P:(k + 1) * P], ident)
                last.then_inc(S["xn_flipped"], 1)
                if True:
                    pe.wait_ge(S["loaded_gate0"], 16)
                pe.wait_ge(S["xnt_copied"], b + 1)
                for t in range(BT):
                    for k in range(KC):
                        last = mm(psL[:, t, :], XB[:, k, t * P:(t + 1) * P], GATE0[:, k, :], start=(k == 0), stop=(k == KC - 1))
                last.then_inc(S["logits_done"], 1)
            pe.wait_ge(S["exp_done"], B)
            with pe.Fori(0, E0 // 2) as i:
                for s in range(2):
                    pe.wait_ge(w_loaded[s], (i + 1) * 16)
                    W13 = WE[:, s, 0:2 * D].rearrange("p (k a c) -> p k a c", k=KC, a=2)
                    W2 = WE[:, s, 2 * D:3 * D]
                    for q in range(2):
                        pe.wait_ge(S["h_done"], (i * 2 + s) * 2 + q)
                        for a in range(2):
                            for k in range(KC):
                                last = mm(PS[:, a, :], W13[:, k, a, :], XNT[:, k, q * 512:(q + 1) * 512],
                                          start=(k == 0), stop=(k == KC - 1))
                        last.then_inc(S["gu_done"], 1)
                        pe.wait_ge(S["h_done"], (i * 2 + s) * 2 + q + 1)
                        for t in range(4):
                            n = q * 4 + t
                            if n < 4:
                                pe.wait_ge(S["o_used"], (i * 2 + s) * TT + (n + 1) - 1)
                            else:
                                pe.wait_ge(S["o_used"], (i * 2 + s) * TT + n - 3)
                            mm(PS[:, 4 + t, 0:D], HH[:, q, t * P:(t + 1) * P], W2,
                               start=True, stop=True).then_inc(S["o_done"], 1)
            pe.wait_ge(S["loaded_l1"], 16 * 7)
            pe.wait_ge(S["o_used"], E0 * TT)
            pe.wait_ge(S["pool_set"], 5)
            with pe.Fori(0, B) as b:
                pe.wait_ge(S["e_xn"], b + 1)
                for k in range(KC):
                    for t in range(BT):
                        last = nc.tensor.transpose(psX3[:, k, t * P:(t + 1) * P], XN[:, t, k * P:(k + 1) * P], ident)
                last.then_inc(S["e_flip"], 1)
                pe.wait_ge(S["e_ctx"], b + 1)
                pe.wait_ge(S["e_xt"], b + 1)
                for g in range(HG):
                    for k in range(KC):
                        mm(psQ[:, g, :], WQ1[:, k, g, :], XB[:, k, :], start=(k == 0), stop=(k == KC - 1))
                pe.wait_ge(S["e_acc"], b * NF)
                for g in range(HG):
                    mm(psK[:, g, :], WKV1[:, 0, g * P:(g + 1) * P], CTB[:, :], start=True, stop=True)
                for t in range(BT):
                    last = mm(PS[:, t, :], CTB[:, t * P:(t + 1) * P], WKV1[:, 1, :], start=True, stop=True)
                last.then_inc(S["e_qkv"], 1)
                pe.wait_ge(S["e_qkv_copied"], b + 1)
                for g in range(HG):
                    if g >= 2:
                        pe.wait_ge(S["e_max"], b * HG + g - 1)
                    for j in range(GH):
                        r = slice(j * HP, (j + 1) * HP)
                        for t in range(BT):
                            dst = ps1[:, g % 2, j, t * P:t * P + (t + 1) * P]
                            mm(dst, QT[r, g, t * P:(t + 1) * P], KT[r, g, 0:(t + 1) * P], start=True, stop=False)
                            last = mm(dst[:, t * P:(t + 1) * P], identb, mask_qk, start=False, stop=True)
                    last.then_inc(S["e_s1"], 1)
                pe.wait_ge(S["e_max"], (b + 1) * HG)
                for t in range(BT):
                    last = nc.tensor.transpose(psM[:, t * P:(t + 1) * P], NM[:, t, :], ident)
                last.then_inc(S["e_flipmax"], 1)
                pe.wait_ge(S["e_mt"], b + 1)
                for g in range(HG):
                    last = mm(psA[:, g, :], sel_max[:, g, :], MT[:, :], start=True, stop=True)
                last.then_inc(S["e_sel"], 1)
                pe.wait_ge(S["e_qm"], b + 1)

                def values(u):
                    pe.wait_ge(S["e_exp"], b * UNITS + u + 1)
                    for i in range(2):
                        g, j = u // 2, u % 2 * 2 + i
                        r = slice(j * HP, (j + 1) * HP)
                        mm(psO[r, g, :], VA[:, 0, g * GH + j, :], PP[:, u % 3, i, 0:N], start=True, stop=False)
                        last = mm(psO[r, g, P:N], VA[:, 1, g * GH + j, :], PP[:, u % 3, i, N:N + P], start=False, stop=True)
                    last.then_inc(S["e_av"], 1)

                for u in range(UNITS):
                    if u >= 3:
                        pe.wait_ge(S["e_exp"], b * UNITS + u - 2)
                    for i in range(2):
                        g, j = u // 2, u % 2 * 2 + i
                        r = slice(j * HP, (j + 1) * HP)
                        dst = ps2[:, u % 3, i, :]
                        mm(dst[:, 0:N], KT[r, g, 0:P], QM[r, g, :], start=True, stop=False)
                        mm(dst[:, 0:P], identb, mask_kq, start=False, stop=True)
                        mm(dst[:, N:N + P], KT[r, g, P:N], QM[r, g, P:N], start=True, stop=False)
                        last = mm(dst[:, N:N + P], identb, mask_kq, start=False, stop=True)
                    last.then_inc(S["e_s2"], 1)
                    if u >= 2:
                        values(u - 2)
                values(UNITS - 2)
                values(UNITS - 1)
                pe.wait_ge(S["e_os"], b + 1)
                for g in range(HG):
                    last = mm(psD[:, g, :], sel_den, OS[:, g, :], start=True, stop=True)
                last.then_inc(S["e_den"], 1)
                pe.wait_ge(S["e_on"], b + 1)
                for t in range(BT):
                    for g in range(HG):
                        last = mm(psY[:, t, :], ON[:, g, t * P:(t + 1) * P], WO1[:, g, :], start=(g == 0), stop=(g == HG - 1))
                last.then_inc(S["e_y"], 1)
                pe.wait_ge(S["e_xn3"], b + 1)
                for k in range(KC):
                    for t in range(BT):
                        last = nc.tensor.transpose(psX3[:, k, t * P:(t + 1) * P], XN[:, t, k * P:(k + 1) * P], ident)
                last.then_inc(S["e_flip3"], 1)
                pe.wait_ge(S["e_xt3"], b + 1)
                for t in range(BT):
                    for k in range(KC):
                        last = mm(psG[:, t, :], XB[:, k, t * P:(t + 1) * P], GATE1[:, k, :], start=(k == 0), stop=(k == KC - 1))
                last.then_inc(S["e_gate"], 1)

                def down(c):
                    pe.wait_ge(S["e_h"], b * NF + c + 1)
                    if c >= 2:
                        pe.wait_ge(S["e_acc"], b * NF + c - 1)
                    for t in range(BT):
                        last = mm(psW[:, c % 2, t, :], H1[:, c % 2, t * P:(t + 1) * P], WD1[:, c, :], start=True, stop=True)
                    last.then_inc(S["e_down"], 1)

                for c in range(NF):
                    if c >= 2:
                        pe.wait_ge(S["e_h"], b * NF + c - 1)
                    for a in range(2):
                        for k in range(KC):
                            last = mm(psGU[:, c % 2, a, :], WGU1[:, c, k, a, :], XB[:, k, :], start=(k == 0), stop=(k == KC - 1))
                    last.then_inc(S["e_gu"], 1)
                    if c:
                        down(c - 1)
                down(NF - 1)

        @block.scalar
        def _(act):
            A = nc.scalar
            act.wait_ge(S["loaded_raw"], 16)
            A.activation(SC[:, 0:1], RAW[:, 0:1], ACT.Tanh, scale=0.5).then_inc(S["tanh_done"], 1)
            A.activation(SC[:, 1:5], RAW[:, 1:5], ACT.Tanh).then_inc(S["tanh_done"], 1)
            with act.Fori(0, B) as b:
                act.wait_ge(S["projected"], b + 1)
                A.copy(QK[:, :, :], psQK).then_inc(S["qk_copied"], 1)
                act.wait_ge(S["scores_done"], b + 1)
                act.wait_ge(S["masked"], b)
                A.mul(SIM[:, :, :], psS, SIM_SCALE).then_inc(S["sim_copied"], 1)
                act.wait_ge(S["sim_copied"], b + 1)
                A.activation(TH[:, :, :], SIM[:, :, :], ACT.Tanh, scale=0.5).then_inc(S["act_mix"], 1)
                act.wait_ge(S["act_mix"], b + 1)
                A.add(TH[:, :, :], TH[:, :, :], 1.0).then_inc(S["th_ready"], 1)
                act.wait_ge(S["xn_flipped"], b + 1)
                A.copy(XNT[:, :, ds(b * N, N)], psX)
                act.wait_ge(S["logits_done"], b)
                A.copy(XB[:, :, :], psX).then_inc(S["xnt_copied"], 1)
                act.wait_ge(S["max_ready"], b + 1)
                for t in range(BT):
                    last = A.activation(EX[:, t, :], LG[:, t, :], ACT.Exp, bias=SM[:, t, 0:1], accum_out=SM[:, t, 1:2])
                last.then_inc(S["exp_done"], 1)
            with act.Fori(0, E0) as e:
                for q in range(2):
                    act.wait_ge(S["gu_done"], e * 2 + q + 1)
                    if q == 0:
                        act.wait_ge(S["h_done"], e * 2)
                    A.activation(SG[:, q, :], PS[:, 0, :], ACT.Silu).then_inc(S["silu_done"], 1)
            with act.Fori(0, B) as b:
                act.wait_ge(S["e_flip"], b + 1)
                A.copy(XB[:, :, :], psX3).then_inc(S["e_xt"], 1)
                act.wait_ge(S["e_qkv"], b + 1)
                A.copy(QT[:, :, :], psQ)
                A.activation(KT[:, :, :], psK, ACT.Identity, bias=k_one)
                A.copy(VA[:, :, :, 0:HD], psV[:, :, :, 0:HD]).then_inc(S["e_qkv_copied"], 1)
                act.wait_ge(S["e_flipmax"], b + 1)
                A.copy(MT[:, :], psM).then_inc(S["e_mt"], 1)
                for u in range(UNITS):
                    act.wait_ge(S["e_s2"], b * UNITS + u + 1)
                    if u >= 3:
                        act.wait_ge(S["e_av"], b * UNITS + u - 2)
                    A.activation(PP[:, u % 3, :, :], ps2[:, u % 3, :, 0:N + P], ACT.Exp, scale=HEAD_SCALE).then_inc(S["e_exp"], 1)
                act.wait_ge(S["e_av"], (b + 1) * UNITS)
                A.copy(OS[:, :, :], psO).then_inc(S["e_os"], 1)
                act.wait_ge(S["e_flip3"], b + 1)
                A.copy(XB[:, :, :], psX3).then_inc(S["e_xt3"], 1)
                act.wait_ge(S["e_gmax"], b + 1)
                for t in range(BT):
                    A.activation(EG[:, t, 0:E1], G14[:, t, 0:E1], ACT.Exp, bias=GS[:, t, 0:1])
                A.activation(EG[:, :, E1:E1 + 1], GS[:, :, 2:3], ACT.Exp, scale=-1.0)
                for t in range(BT):
                    last = A.activation(EG[:, t, E1 + 1:E1 + 2], TP[:, t, 1:2], ACT.Exp, bias=GS[:, t, 0:1])
                last.then_inc(S["e_gexp"], 1)
                for c in range(NF):
                    act.wait_ge(S["e_gu"], b * NF + c + 1)
                    if c >= 2:
                        act.wait_ge(S["e_h"], b * NF + c - 1)
                    A.activation(SG1[:, c % 2, :], psGU[:, c % 2, 0, :], ACT.Silu).then_inc(S["e_silu"], 1)

        @block.vector
        def _(dve):
            V = nc.vector
            st = Steps(dve, S["dve_scalar"])
            dve.wait_ge(S["tanh_done"], 2)
            st.done(V.tensor_scalar(SC[:, 5:6], SC[:, 0:1], 1.0, 0.125, ALU.add, ALU.mult))
            st.done(V.tensor_scalar(SC[:, 6:7], SC[:, 0:1], -0.5, 0.5, ALU.mult, ALU.add))
            st.wait()
            st.done(V.tensor_tensor(SC[:, 5:6], SC[:, 5:6], SC[:, 1:2], ALU.mult))
            st.done(V.tensor_tensor(SC[:, 6:7], SC[:, 6:7], SC[:, 1:2], ALU.mult))
            st.wait()
            st.end()
            c_graph, c_norm = SC[:, 5:6], SC[:, 6:7]
            c_ffn0, c_att1, c_ffn1 = SC[:, 3:4], SC[:, 2:3], SC[:, 4:5]

            def norm_stats(st, src):
                for t in range(BT):
                    st.done(V.bn_stats(ST[:, t, :], src(t)))
                st.wait()
                for t in range(BT):
                    st.done(V.bn_aggr(MV[:, t, :], ST[:, t, :]))
                st.wait()
                v, y, h = RS[:, :, 3:4], RS[:, :, 0:1], RS[:, :, 4:5]
                st.done(V.tensor_scalar(v, MV[:, :, 1:2], EPS, None, ALU.add))
                st.wait()
                st.done(V.tensor_scalar(y.bitcast(I32), v.bitcast(I32), -0.5, RSQRT_GUESS, ALU.mult, ALU.add))
                for _ in range(NEWTON):
                    st.wait()
                    st.done(V.scalar_tensor_tensor(h, y, -0.5, y, ALU.mult, ALU.mult))
                    st.wait()
                    st.done(V.tensor_tensor(h, h, v, ALU.mult))
                    st.wait()
                    st.done(V.scalar_tensor_tensor(y, h, 1.5, y, ALU.add, ALU.mult))
                st.wait()

            def norm(st, src):
                norm_stats(st, lambda t: src[:, t, :])
                for t in range(BT):
                    last = V.tensor_scalar(XN[:, t, :], src[:, t, :], MV[:, t, 0:1], RS[:, t, 0:1], ALU.subtract, ALU.mult)
                return last

            dve.wait_ge(S["loaded_x"], 16)
            with dve.Fori(0, B) as b:
                st = Steps(dve, S["dve_mix"])
                norm_stats(st, lambda t: X[:, ds(b * BT + t, 1), :])
                st.done(V.tensor_scalar(RS[:, :, 1:2], RS[:, :, 0:1], c_norm, None, ALU.mult))
                st.wait()
                st.done(V.scalar_tensor_tensor(RS[:, :, 2:3], MV[:, :, 0:1], -1.0, RS[:, :, 1:2], ALU.mult, ALU.mult))
                st.wait()
                dve.wait_ge(S["sim_copied"], b + 1)
                for t in range(BT):
                    last = V.tensor_scalar(BASE[:, t, :], X[:, ds(b * BT + t, 1), :], RS[:, t, 1:2], RS[:, t, 2:3], ALU.mult, ALU.add)
                    st.done(last)
                for r in range(ROUNDS):
                    src = SIM if r == 0 else WORK
                    for t in range(BT):
                        if r:
                            st.wait(1)
                        st.done(V.max(TOP[:, t, :], src[:, t, :]))
                    if r < ROUNDS - 1:
                        for t in range(BT):
                            st.wait(1)
                            st.done(V.match_replace(WORK[:, t, :], TOP[:, t, :], src[:, t, :], LOWEST))
                st.wait()
                k = (KTH - 1) % 8
                dve.wait_ge(S["th_ready"], b + 1)
                for t in range(BT):
                    last = V.scalar_tensor_tensor(AM[:, t, :], SIM[:, t, :], TOP[:, t, k:k + 1], TH[:, t, :], ALU.is_ge, ALU.mult)
                last.then_inc(S["masked"], 1)
                dve.wait_ge(S["masked"], b + 1)
                Xb = X[:, ds(b * BT, BT), :]
                st.done(V.tensor_tensor(BASE[:, :, :], BASE[:, :, :], Xb, ALU.add))
                st.wait()
                st.done(V.scalar_tensor_tensor(XW[:, :, :], AM[:, :, :], c_graph, BASE[:, :, :], ALU.mult, ALU.add))
                st.wait()
                dve.wait_ge(S["flipped"], b + 1)
                st.done(V.scalar_tensor_tensor(XW[:, :, :], psT, c_graph, XW[:, :, :], ALU.mult, ALU.add))
                st.wait()
                norm(st, XW).then_inc(S["xn_ready"], 1)
                st.done(V.tensor_copy(X1[:, ds(b * BT, BT), :], XW[:, :, :]))
                dve.wait_ge(S["logits_done"], b + 1)
                st.done(V.tensor_copy(LG[:, :, :], psL))
                st.wait()
                for t in range(BT):
                    st.done(V.max(L8[:, t, :], LG[:, t, :]))
                st.wait()
                V.tensor_scalar(SM[:, :, 0:1], L8[:, :, 0:1], -1.0, None, ALU.mult).then_inc(S["max_ready"], 1)
                for t in range(BT):
                    st.done(V.match_replace(LR[:, t, :], L8[:, t, :], LG[:, t, :], LOWEST))
                st.wait()
                st.done(V.tensor_tensor(LR[:, :, :], LG[:, :, :], LR[:, :, :], ALU.not_equal))
                dve.wait_ge(S["exp_done"], b + 1)
                st.done(V.reciprocal(SM[:, :, 2:3], SM[:, :, 1:2]))
                st.wait()
                for t in range(BT):
                    st.done(V.scalar_tensor_tensor(C0[:, ds(b * BT + t, 1), :], EX[:, t, :], SM[:, t, 2:3], LR[:, t, :], ALU.mult, ALU.mult))
                st.wait()
                st.end()
            dve.wait_ge(S["pool_set"], 5)
            with dve.Fori(0, E0) as e:
                for q in range(2):
                    dve.wait_ge(S["silu_done"], e * 2 + q + 1)
                    if q == 0:
                        dve.wait_ge(S["o_done"], e * TT)
                    V.tensor_tensor(HH[:, q, :], SG[:, q, :], PS[:, 1, :], ALU.mult).then_inc(S["h_done"], 1)
                    for t in range(4):
                        n = q * 4 + t
                        dve.wait_ge(S["o_done"], e * TT + n + 1)
                        V.scalar_tensor_tensor(MOE[:, n, :], PS[:, 4 + t, 0:D], C0[:, n, ds(e, 1)], MOE[:, n, :],
                                               ALU.mult, ALU.add).then_inc(S["o_used"], 1)
            dve.wait_ge(S["o_used"], E0 * TT)
            with dve.Fori(0, B) as b:
                st = Steps(dve, S["dve_l1"])
                st.done(V.scalar_tensor_tensor(X2[:, :, :], MOE[:, ds(b * BT, BT), :], c_ffn0, X1[:, ds(b * BT, BT), :], ALU.mult, ALU.add))
                st.wait()
                norm(st, X2).then_inc(S["e_xn"], 1)
                for g in range(HG):
                    dve.wait_ge(S["e_s1"], b * HG + g + 1)
                    for t in range(BT):
                        last = V.tensor_reduce(NM[:, t, g * GH:(g + 1) * GH], ps1[:, g % 2, :, t * P:t * P + (t + 1) * P],
                                               AX.X, ALU.max, negate=True)
                    last.then_inc(S["e_max"], 1)
                dve.wait_ge(S["e_sel"], b + 1)
                V.tensor_tensor(QM[:, :, :], psA, QT[:, :, :], ALU.add).then_inc(S["e_qm"], 1)
                dve.wait_ge(S["e_den"], b + 1)
                st.done(V.reciprocal(RD[:, :, :], psD))
                st.wait()
                V.tensor_tensor(ON[:, :, :], OS[:, :, :], RD[:, :, :], ALU.mult).then_inc(S["e_on"], 1)
                dve.wait_ge(S["e_y"], b + 1)
                st.done(V.scalar_tensor_tensor(X3[:, :, :], psY, c_att1, X2[:, :, :], ALU.mult, ALU.add))
                st.wait()
                norm(st, X3).then_inc(S["e_xn3"], 1)
                dve.wait_ge(S["e_gate"], b + 1)
                st.done(V.tensor_copy(G14[:, :, 0:E1], psG[:, :, 0:E1]))
                st.done(V.tensor_copy(GS[:, :, 2:3], psG[:, :, E1:E1 + 1]))
                st.wait()
                for t in range(BT):
                    st.done(V.max(T8[:, t, :], G14[:, t, 0:E1]))
                st.wait()
                st.done(V.tensor_copy(TP[:, :, 0:2], T8[:, :, 0:2]))
                st.done(V.tensor_scalar(GS[:, :, 0:1], T8[:, :, 0:1], -1.0, None, ALU.mult))
                st.wait()
                V.tensor_scalar(GS[:, :, 1:2], T8[:, :, 0:1], 1.0, None, ALU.mult).then_inc(S["e_gmax"], 1)
                for t in range(BT):
                    st.done(V.match_replace(G14R[:, t, 0:14], TP[:, t, :], G14[:, t, 0:14], LOWEST))
                st.wait()
                st.done(V.tensor_tensor(G14R[:, :, 0:E1], G14[:, :, 0:E1], G14R[:, :, 0:E1], ALU.not_equal))
                dve.wait_ge(S["e_gexp"], b + 1)
                st.done(V.tensor_scalar(EG[:, :, E1:E1 + 2], EG[:, :, E1:E1 + 2], 1.0, None, ALU.add))
                st.wait()
                st.done(V.reciprocal(EG[:, :, E1 + 2:E1 + 4], EG[:, :, E1:E1 + 2]))
                st.wait()
                st.done(V.tensor_copy(CM[:, :, E1:E1 + 1], EG[:, :, E1 + 2:E1 + 3]))
                for t in range(BT):
                    st.done(V.scalar_tensor_tensor(CM[:, t, 0:E1], EG[:, t, 0:E1], EG[:, t, E1 + 3:E1 + 4], G14R[:, t, 0:E1],
                                                   ALU.mult, ALU.mult))
                st.wait()

                def add_up(c):
                    dve.wait_ge(S["e_down"], b * NF + c + 1)
                    for t in range(BT):
                        w = CM[:, t, min(c, E1):min(c, E1) + 1]
                        if c == 0:
                            last = V.tensor_scalar(FA[:, t, :], psW[:, c % 2, t, :], w, None, ALU.mult)
                        else:
                            last = V.scalar_tensor_tensor(FA[:, t, :], psW[:, c % 2, t, :], w, FA[:, t, :], ALU.mult, ALU.add)
                    last.then_inc(S["e_acc"], 1)

                for c in range(NF):
                    dve.wait_ge(S["e_silu"], b * NF + c + 1)
                    if c >= 2:
                        dve.wait_ge(S["e_down"], b * NF + c - 1)
                    V.tensor_tensor(H1[:, c % 2, :], SG1[:, c % 2, :], psGU[:, c % 2, 1, :], ALU.mult).then_inc(S["e_h"], 1)
                    if c:
                        if c > 1:
                            dve.wait_ge(S["e_acc"], b * NF + c - 1)
                        add_up(c - 1)
                dve.wait_ge(S["e_acc"], b * NF + NF - 1)
                add_up(NF - 1)
                dve.wait_ge(S["e_acc"], (b + 1) * NF)
                dve.wait_ge(S["stored"], b * 16)
                V.scalar_tensor_tensor(OUT[:, :, :], FA[:, :, :], c_ffn1, X3[:, :, :], ALU.mult, ALU.add).then_inc(S["e_out"], 1)
                st.end()


def kernel(**inputs):
    import ml_dtypes
    import numpy as np
    import concourse.bacc as bacc
    from concourse.bass_utils import run_bass_kernel_spmd

    def at(name):
        return np.asarray(inputs[name])

    def pad_heads(w):
        k = w.shape[0]
        padded = np.zeros((k, NH, HP), w.dtype)
        padded[:, :, :HD] = w.reshape(k, NH, HD)
        return padded.reshape(k, NH * HP)

    def chunks(w):
        return w.reshape(-1, P, w.shape[-1]).transpose(1, 0, 2)

    w13, w2 = at("L0_ffn_w13"), at("L0_ffn_w2")
    w13T = w13.transpose(0, 2, 1).reshape(E0, KC, P, 2 * I0).transpose(0, 2, 1, 3).reshape(E0, P, KC * 2 * I0)
    wexp = np.concatenate([w13T, w2.transpose(0, 2, 1)], axis=2).reshape(E0 * P, 3 * D)
    wkv = at("L1_xattn_Wkv_expand").T
    gate = np.concatenate([at("L1_ffn_w_gate"), at("L1_ffn_sh_gate").reshape(2, P, D)])
    up = np.concatenate([at("L1_ffn_w_up"), at("L1_ffn_sh_up").reshape(2, P, D)])
    gu = np.stack([gate, up], axis=1)
    wgu = gu.reshape(NF, 2, P, KC, P).transpose(4, 0, 3, 1, 2)
    down = np.concatenate([at("L1_ffn_w_down").transpose(0, 2, 1), at("L1_ffn_sh_down").T.reshape(2, P, D)])
    raw = np.concatenate([at("L0_xattn_gamma_raw").reshape(1), at("g_xattn"), at("g_ffn")])[None, :]

    row, col = np.arange(P)[:, None], np.arange(P)[None, :]
    cf = np.zeros((P, 2 * P + HG * P + 1), np.float32)
    cf[:, 0:P] = np.eye(P)
    cf[:, P:2 * P] = row == col // HP * HP + HD
    for h in range(NH):
        cf[h, 2 * P + h * HP + HD] = 1.0
    cf[:, -1] = np.arange(P) % HP == HD
    cb = np.zeros((P, 5, P), ml_dtypes.bfloat16)
    cb[:, 0] = np.eye(P)
    cb[:, 1] = np.where(col > row, -1.0e38, 0.0)
    cb[:, 2] = np.where(row > col, -1.0e38, 0.0)
    cb[:, 3] = row < col
    cb[:, 4] = 1.0

    ins = {
        "x": at("x").reshape(T, D),
        "ctxT": at("ctx_512").reshape(T, DC).T,
        "raw": raw,
        "wqk0": np.pad(np.stack([at("L0_xattn_Wq").T, at("L0_xattn_Wk").T], axis=1), ((0, 0), (0, 0), (0, P - DC))),
        "gate0": chunks(at("L0_ffn_gate_w").T),
        "wexp": wexp,
        "wq1": chunks(pad_heads(at("L1_xattn_Wq").T)).reshape(P, KC, HG, P),
        "wkv1": np.stack([pad_heads(wkv[:, :D]), pad_heads(wkv[:, D:])], axis=1),
        "wo1": pad_heads(at("L1_xattn_Wout")).T.reshape(HG, P, D).transpose(1, 0, 2),
        "gate1": chunks(np.concatenate([at("L1_ffn_gate_w"), at("L1_ffn_se_gate_w")]).T),
        "wgu1": wgu,
        "wd1": down.transpose(1, 0, 2),
        "cf": cf,
        "cb": cb,
    }
    nc = bacc.Bacc("TRN2", target_bir_lowering=False, num_devices=1)
    arrays, args = {}, []
    for name, a in ins.items():
        a = np.ascontiguousarray(a)
        arrays[f"in_{name}"] = a
        args.append(nc.dram_tensor(f"in_{name}", a.shape, mybir.dt.from_np(a.dtype), kind="ExternalInput").ap())
    args.append(nc.dram_tensor("out_0", (T, D), F32, kind="ExternalOutput").ap())
    gated_block(nc, *args)
    r = run_bass_kernel_spmd(nc, [arrays], core_ids=[0])
    return r.results[0]["out_0"].reshape(B, N, D)
```

```python
from contextlib import ExitStack

import concourse.bass as bass
from concourse import mybir

F32 = mybir.dt.float32
BF16 = mybir.dt.bfloat16
I32 = mybir.dt.int32
ACT = mybir.ActivationFunctionType
ALU = mybir.AluOpType
AX = mybir.AxisListType
ds = bass.ds

P = 128
B, N, D = 4, 256, 256
DC = 64
T = B * N
TT = T // P
BT = N // P
KC = D // P
E0, TOP0 = 64, 8
I0 = 128
CAP = 192
SP_ = CAP // 2
SLOTS = E0 * CAP
SKIP = 65536.0
RING = 12
PEEL = 3
KTH = int(N * 0.3)
ROUNDS = (KTH + 7) // 8
NH, HD = 16, 16
HP = 32
HG, GH = NH * HP // P, P // HP
UNITS = NH // 2
E1 = 8
NF = E1 + 2
EPS = 1e-5
RSQRT_GUESS = float(0x5F3759DF)
NEWTON = 3
NORM_STEPS = 2 * BT + 2 + 3 * NEWTON
LOWEST = -3.0e38
SIM_SCALE = 1.0 / 16.0
HEAD_SCALE = HD ** -0.5


class Steps:

    def __init__(self, eng, sem):
        self.eng, self.sem, self.n = eng, sem, 0

    def done(self, ins):
        self.n += 1
        ins.then_inc(self.sem, 1)

    def wait(self, behind=0):
        self.eng.wait_ge(self.sem, self.n - behind)

    def end(self):
        self.wait()
        self.eng.sem_clear(self.sem)
        self.n = 0


def gated_block(nc, xs, ys, x, ctxT, raw, wqk0, gate0, wexp, wq1, wkv1, wo1, gate1, wgu1, wd1, cf, cb, out):
    with ExitStack() as ctx:
        def sb(name, shape, dt=F32):
            return ctx.enter_context(nc.sbuf_tensor(name, shape, dt))

        def sem(name):
            return ctx.enter_context(nc.semaphore(name))

        X = sb("X", [P, TT, D])
        CT = sb("CT", [DC, T])
        WQK0 = sb("WQK0", [DC, 2, P])
        GATE0 = sb("GATE0", [P, KC, E0])
        WQ1 = sb("WQ1", [P, KC, HG, P])
        WKV1 = sb("WKV1", [DC, 2, HG * P])
        WO1 = sb("WO1", [P, HG, D])
        GATE1 = sb("GATE1", [P, KC, E1 + 1])
        WGU1 = sb("WGU1", [P, NF, KC, 2, P])
        WD1 = sb("WD1", [P, NF, D])
        CF = sb("CF", [P, 2 * P + HG * P + 1 + BT * E0])
        CB = sb("CB", [P, 5, P], BF16)
        ident, sel_den = CF[:, 0:P], CF[:, P:2 * P]
        sel_max = CF[0:NH, 2 * P:2 * P + HG * P].rearrange("p (g c) -> p g c", g=HG)
        k_one = CF[:, 2 * P + HG * P:2 * P + HG * P + 1]
        slot_base = CF[:, 2 * P + HG * P + 1:].rearrange("p (t e) -> p t e", t=BT)
        identb, mask_qk, mask_kq, before, onesb = (CB[:, i, :] for i in range(5))
        RAW = sb("RAW", [P, 5])
        SC = sb("SC", [P, 8])
        X1 = sb("X1", [P, TT, D])
        XNT = sb("XNT", [P, KC, T])
        C0 = sb("C0", [P, TT, E0])
        MOE = sb("MOE", [P, TT, D])
        XNA = sb("XNA", [P, TT, D])
        KEY = sb("KEY", [P, TT, E0])
        C0M = sb("C0M", [P, TT, E0])
        C0X = sb("C0X", [P, TT, E0])
        K8 = sb("K8", [P, TT, TOP0])
        IDX = sb("IDX", [P, TT, TOP0], I32)
        W8 = sb("W8", [P, TT, TOP0])
        QK = sb("QK", [P, 2, N])
        SIM = sb("SIM", [P, BT, N])
        TH = sb("TH", [P, BT, N])
        WORK = sb("WORK", [P, BT, N])
        TOP = sb("TOP", [P, BT, 8])
        AM = sb("AM", [P, BT, N])
        BASE = sb("BASE", [P, BT, N])
        XW = sb("XW", [P, BT, D])
        XN = sb("XN", [P, BT, D])
        ST = sb("ST", [P, BT, 6])
        MV = sb("MV", [P, BT, 2])
        RS = sb("RS", [P, BT, 8])
        XB = sb("XB", [P, KC, N])
        LG = sb("LG", [P, BT, E0])
        LR = sb("LR", [P, BT, E0])
        MB = sb("MB", [P, BT, E0], BF16)
        MA = sb("MA", [P, E0], BF16)
        OV = sb("OV", [P, BT, E0])
        K1 = sb("K1", [P, BT, E0])
        KW = sb("KW", [P, BT, 8])
        FM = sb("FM", [P, 1])
        FLAG = sb("FLAG", [P, 1], I32)
        EQ = sb("EQ", [P, TOP0, E0])
        EX = sb("EX", [P, BT, E0])
        L8 = sb("L8", [P, BT, 8])
        SM = sb("SM", [P, BT, 4])
        WR = sb("WR", [P, RING, 3 * D])
        XE = sb("XE", [SP_, 3, 2, D])
        XTE = sb("XTE", [P, 2, KC, CAP])
        SGE = sb("SGE", [P, 2, CAP])
        HE = sb("HE", [P, 2, CAP])
        OE = sb("OE", [SP_, 3, 2, D])
        GB = sb("GB", [P, BT, TOP0, D])
        WE = WR
        ZERO = GB[:, 0, :, :].rearrange("p j d -> p (j d)")
        SG = GB[:, 0, 0:4, :].rearrange("p (q k) n -> p q (k n)", q=2)
        HH = GB[:, 0, 4:8, :].rearrange("p (q k) n -> p q (k n)", q=2)
        CTB = sb("CTB", [DC, N])
        X2, X3, FA, OUT, SG1, H1 = BASE, SIM, TH, WORK, AM, XW
        QT, KT, QM, OS, RD, ON = (WR[:, :, :].rearrange("p s c -> p (s c)")[:, i * HG * N:(i + 1) * HG * N]
                                  .rearrange("p (g n) -> p g n", g=HG) for i in range(6))
        PP = WR[:, 8:11, :].rearrange("p u (h n) -> p u h n", h=2)
        VA = sb("VA", [P, BT, NH, HP])
        NM = sb("NM", [P, BT, NH])
        MT = sb("MT", [NH, N])
        G14 = sb("G14", [P, BT, 16])
        G14R = sb("G14R", [P, BT, 16])
        TP = sb("TP", [P, BT, 8])
        T8 = sb("T8", [P, BT, 8])
        EG = sb("EG", [P, BT, 16])
        CM = sb("CM", [P, BT, E1 + 1])
        GS = sb("GS", [P, BT, 8])

        PS = ctx.enter_context(nc.psum_tensor("PS", [P, 8, 512], F32))

        def bank(i, **dims):
            shape = PS[:, i, :]
            return shape

        psQK = PS[:, 0, :].rearrange("p (a n) -> p a n", a=2)
        psS = PS[:, 1, :].rearrange("p (a n) -> p a n", a=2)
        psT = PS[:, 2, :].rearrange("p (a n) -> p a n", a=2)
        psX = PS[:, 3, :].rearrange("p (a n) -> p a n", a=2)
        psL = PS[:, 4, 0:BT * E0].rearrange("p (a n) -> p a n", a=BT)
        psR = PS[:, 5, 0:BT * E0].rearrange("p (a n) -> p a n", a=BT)
        psN = PS[:, 6, 0:E0]
        psXE = [PS[:, i, 0:KC * CAP].rearrange("p (k n) -> p k n", k=KC) for i in range(2)]
        psGE = [PS[:, 2 + i, 0:2 * CAP].rearrange("p (a n) -> p a n", a=2) for i in range(2)]
        psOE = [PS[0:SP_, 4 + i, :].rearrange("p (r n) -> p r n", r=2) for i in range(2)]
        ps1 = PS[:, :, :].rearrange("p (s h) c -> p s h c", s=2)
        ps2 = PS[:, 0:6, :].rearrange("p (s h) c -> p s h c", s=3)
        psO = PS[:, 6:8, :].rearrange("p b (g n) -> p (b g) n", g=2)
        psQ = PS[:, 4:6, :].rearrange("p b (g n) -> p (b g) n", g=2)
        psK = PS[:, 6:8, :].rearrange("p b (g n) -> p (b g) n", g=2)
        psV = PS[:, 0:2, :].rearrange("p t (h c) -> p t h c", h=NH)
        psX3 = PS[:, 3, :].rearrange("p (a n) -> p a n", a=2)
        psM = PS[0:NH, 0, 0:N]
        psA = PS[:, 6:8, :].rearrange("p b (g n) -> p (b g) n", g=2)
        psD = PS[:, 0:2, :].rearrange("p b (g n) -> p (b g) n", g=2)
        psY = PS[:, 2, :].rearrange("p (a n) -> p a n", a=2)
        psG = PS[:, 2, 0:BT * (E1 + 1)].rearrange("p (a n) -> p a n", a=BT)
        psGU = PS[:, 4:6, :].rearrange("p s (a n) -> p s a n", a=2)
        psW = PS[:, 6:8, :].rearrange("p s (a n) -> p s a n", a=2)

        names = """loaded_ctx loaded_x loaded_raw loaded_gate0 loaded_l1 tanh_done scalars_done
            projected qk_copied scores_done sim_copied th_ready masked flipped xn_ready xn_flipped
            xnt_copied logits_done max_ready exp_done dve_scalar dve_mix act_mix x1_kept
            gu_done silu_done h_done o_done o_used
            zero_set zeroed mask_ready ranked xna_ready idx_ready scattered counted flag_ready w8_ready
            all_stored general_done gb_used xt_flipped xt_copied gue_done silue_done he_done oe_done oe_copied dve_w8
            e_ctx e_xn e_flip e_xt e_qkv e_qkv_copied e_s1 e_max e_flipmax e_mt e_sel
            e_qm e_s2 e_exp e_av e_os e_den e_on e_y e_xn3 e_flip3 e_xt3 e_gate e_gmax e_gexp
            e_gu e_silu e_h e_down e_acc e_out dve_l1 pool_set stored""".split()
        S = {n: sem(n) for n in names}
        w_loaded = [sem(f"w_loaded{i}") for i in range(2)]
        wr_loaded = [sem(f"wr_loaded{i}") for i in range(RING)]
        xe_loaded = [sem(f"xe_loaded{i}") for i in range(3)]
        oe_stored = [sem(f"oe_stored{i}") for i in range(3)]
        gathered = [sem(f"gathered{i}") for i in range(BT)]

        def expert_steps(eng, step, first, last):
            for e in first:
                step(0, e)
            with eng.Fori(0, (E0 - 4) // RING) as turn:
                for u in range(RING):
                    step(turn, PEEL + u)
            for e in last:
                step(0, e)

        def uses(turn, place, ring):
            return turn * (RING // ring) + place // ring

        def reused(turn, place, ring):
            return place >= ring or not isinstance(turn, int)

        block = ctx.enter_context(nc.Block())

        @block.sync
        def _(sp):
            sp.dma_start(CT[:, :], ctxT).then_inc(S["loaded_ctx"], 16)
            sp.dma_start(WQK0[:, :, :], wqk0).then_inc(S["loaded_ctx"], 16)
            sp.dma_start(CF[:, :], cf).then_inc(S["loaded_ctx"], 16)
            sp.dma_start(X[:, :, :], x.rearrange("(t p) d -> p t d", p=P)).then_inc(S["loaded_x"], 16)
            sp.dma_start(RAW[:, :], raw.to_broadcast([P, 5])).then_inc(S["loaded_raw"], 16)
            sp.dma_start(GATE0[:, :, :], gate0).then_inc(S["loaded_gate0"], 16)
            sp.dma_start(CB[:, :, :], cb).then_inc(S["loaded_gate0"], 16)
            sp.wait_ge(S["zero_set"], 1)
            for i in range(SLOTS // (8 * P)):
                sp.dma_start(xs[i * 8 * P:(i + 1) * 8 * P, :].rearrange("(p r) d -> p (r d)", p=P), ZERO)\
                  .then_inc(S["zeroed"], 16)
            for dst, src in ((WQ1[:, :, :, :], wq1), (WKV1[:, :, :], wkv1), (WO1[:, :, :], wo1),
                             (GATE1[:, :, :], gate1), (WGU1[:, :, :, :, :], wgu1), (WD1[:, :, :], wd1)):
                sp.dma_start(dst, src).then_inc(S["loaded_l1"], 16)
            for i in range(RING):
                sp.dma_start(WR[:, i, :], wexp[i * P:(i + 1) * P, :]).then_inc(wr_loaded[i], 16)

            def load_slots(turn, place):
                e = turn * RING + place
                sp.dma_start(XE[:, place % 3, :, :], xs[ds(e * CAP, CAP), :].rearrange("(p r) d -> p r d", r=2))\
                  .then_inc(xe_loaded[place % 3], 16)

            def store_slots(turn, place):
                e = turn * RING + place
                sp.wait_ge(S["oe_copied"], e + 1)
                sp.dma_start(ys[ds(e * CAP, CAP), :].rearrange("(p r) d -> p r d", r=2), OE[:, place % 3, :, :])\
                  .then_inc(oe_stored[place % 3], 16)

            sp.wait_ge(S["scattered"], 16 * TT * TOP0)
            for e in range(3):
                load_slots(0, e)

            def step(turn, place):
                e = turn * RING + place
                fixed = isinstance(turn, int)
                if not fixed or e + 2 < E0:
                    sp.wait_ge(S["xt_flipped"], e)
                    load_slots(turn, place + 2)
                store_slots(turn, place - 1)
                if not fixed or e - 1 + RING < E0:
                    sp.dma_start(WR[:, (place - 1) % RING, :], wexp[ds((e + (RING - 1)) * P, P), :])\
                      .then_inc(wr_loaded[(place - 1) % RING], 16)

            for e in range(1, PEEL):
                step(0, e)
            with sp.Fori(0, 4) as turn:
                for u in range(RING):
                    step(turn, PEEL + u)
            for e in range(PEEL + 4 * RING, E0 + 1):
                step(0, e)
            for i in range(3):
                sp.wait_ge(oe_stored[i], 16 * len(range(i, E0, 3)))
            sp.sem_inc(S["all_stored"], 1)
            sp.wait_ge(S["flag_ready"], 1)
            with sp.If(sp.value_load(FLAG[0:1, 0:1])):
                sp.wait_ge(S["he_done"], E0)
                for s in range(2):
                    sp.dma_start(WE[:, s, :], wexp[s * P:(s + 1) * P, :]).then_inc(w_loaded[s], 16)
                with sp.Fori(1, E0 // 2) as i:
                    for s in range(2):
                        sp.wait_ge(S["o_done"], (i * 2 + s - 1) * TT)
                        sp.dma_start(WE[:, s, :], wexp[ds(i * (2 * P) + s * P, P), :]).then_inc(w_loaded[s], 16)
            with sp.Fori(0, B) as b:
                sp.wait_ge(S["e_out"], b + 1)
                sp.dma_start(out[ds(b * N, N), :].rearrange("(t p) d -> p t d", p=P), OUT[:, :, :]).then_inc(S["stored"], 16)
            sp.wait_ge(S["stored"], 16 * B)

        @block.gpsimd
        def _(pool):
            nc.gpsimd.memset(VA[:, :, :, :], 0.0).then_inc(S["pool_set"], 1)
            pool.wait_ge(S["pool_set"], 1)
            nc.gpsimd.memset(VA[:, :, :, HD:HD + 1], 1.0).then_inc(S["pool_set"], 1)
            nc.gpsimd.memset(MOE[:, :, :], 0.0).then_inc(S["pool_set"], 1)
            nc.gpsimd.memset(G14[:, :, :], 1.0e30).then_inc(S["pool_set"], 1)
            nc.gpsimd.memset(TP[:, :, :], 1.0e30).then_inc(S["pool_set"], 1)
            pool.wait_ge(S["zeroed"], 16 * (SLOTS // (8 * P)))
            for t in range(TT):
                pool.wait_ge(S["xna_ready"], t // BT + 1)
                pool.wait_ge(S["idx_ready"], t // BT + 1)
                for j in range(TOP0):
                    pool.indirect_dma_start(out=xs, out_offset=bass.IndirectOffsetOnAxis(ap=IDX[:, t, j:j + 1], axis=0),
                                            in_=XNA[:, t, :], in_offset=None, bounds_check=SLOTS - 1, oob_is_err=False)\
                        .then_inc(S["scattered"], 16)
            pool.wait_ge(S["pool_set"], 5)
            pool.wait_ge(S["all_stored"], 1)
            pool.wait_ge(S["general_done"], 1)

            def gather(t):
                for j in range(TOP0):
                    pool.indirect_dma_start(out=GB[:, t % BT, j, :], out_offset=None, in_=ys,
                                            in_offset=bass.IndirectOffsetOnAxis(ap=IDX[:, t, j:j + 1], axis=0),
                                            bounds_check=SLOTS - 1, oob_is_err=False).then_inc(gathered[t % BT], 16)

            for b in range(B):
                for i in range(BT):
                    pool.wait_ge(S["gb_used"], b * BT + i)
                    gather(b * BT + i)
                pool.wait_ge(S["e_qkv"], b)
                nc.gpsimd.tensor_copy(CTB[:, :], CT[:, b * N:(b + 1) * N]).then_inc(S["e_ctx"], 1)

        @block.tensor
        def _(pe):
            mm = nc.tensor.matmul
            pe.wait_ge(S["loaded_ctx"], 48)
            with pe.Fori(0, B) as b:
                pe.wait_ge(S["qk_copied"], b)
                for a in range(2):
                    last = mm(psQK[:, a, :], WQK0[:, a, :], CT[:, ds(b * N, N)], start=True, stop=True)
                last.then_inc(S["projected"], 1)
                pe.wait_ge(S["qk_copied"], b + 1)
                pe.wait_ge(S["sim_copied"], b)
                for t in range(BT):
                    last = mm(psS[:, t, :], QK[:, 0, t * P:(t + 1) * P], QK[:, 1, :], start=True, stop=True)
                last.then_inc(S["scores_done"], 1)
                pe.wait_ge(S["masked"], b + 1)
                for t in range(BT):
                    for c in range(BT):
                        last = nc.tensor.transpose(psT[:, t, c * P:(c + 1) * P], AM[:, c, t * P:(t + 1) * P], ident)
                last.then_inc(S["flipped"], 1)
                pe.wait_ge(S["xn_ready"], b + 1)
                for k in range(KC):
                    for t in range(BT):
                        last = nc.tensor.transpose(psX[:, k, t * P:(t + 1) * P], XN[:, t, k * P:(k + 1) * P], ident)
                last.then_inc(S["xn_flipped"], 1)
                if True:
                    pe.wait_ge(S["loaded_gate0"], 32)
                pe.wait_ge(S["xnt_copied"], b + 1)
                for t in range(BT):
                    for k in range(KC):
                        last = mm(psL[:, t, :], XB[:, k, t * P:(t + 1) * P], GATE0[:, k, :], start=(k == 0), stop=(k == KC - 1))
                last.then_inc(S["logits_done"], 1)
                pe.wait_ge(S["mask_ready"], b + 1)
                for t in range(BT):
                    mm(psR[:, t, :], before, MB[:, t, :], start=True, stop=False)
                    if t:
                        mm(psR[:, t, :], onesb, MB[:, 0, :], start=False, stop=False)
                    last = mm(psR[:, t, :], onesb, MA[:, :], start=False, stop=True)
                last.then_inc(S["ranked"], 1)
            pe.wait_ge(S["idx_ready"], B)
            mm(psN, onesb, MA[:, :], start=True, stop=True).then_inc(S["counted"], 1)

            def flip(turn, place):
                e = turn * RING + place
                pe.wait_ge(xe_loaded[place % 3], uses(turn, place, 3) * 16 + 16)
                if reused(turn, place, 2):
                    pe.wait_ge(S["xt_copied"], e - 1)
                for k in range(KC):
                    for r in range(2):
                        last = nc.tensor.transpose(psXE[place % 2][:, k, r * SP_:(r + 1) * SP_],
                                                   XE[:, place % 3, r, k * P:(k + 1) * P], ident[0:SP_, 0:SP_])
                last.then_inc(S["xt_flipped"], 1)

            def gate_up(turn, place):
                e = turn * RING + place
                pe.wait_ge(S["xt_copied"], e + 1)
                pe.wait_ge(wr_loaded[place % RING], uses(turn, place, RING) * 16 + 16)
                if reused(turn, place, 2):
                    pe.wait_ge(S["he_done"], e - 1)
                W13 = WR[:, place % RING, 0:2 * D].rearrange("p (k a c) -> p k a c", k=KC, a=2)
                for a in range(2):
                    for k in range(KC):
                        last = mm(psGE[place % 2][:, a, :], W13[:, k, a, :], XTE[:, place % 2, k, :], start=(k == 0), stop=(k == KC - 1))
                last.then_inc(S["gue_done"], 1)

            def down_slots(turn, place):
                e = turn * RING + place
                pe.wait_ge(S["he_done"], e + 1)
                if reused(turn, place, 2):
                    pe.wait_ge(S["oe_copied"], e - 1)
                for r in range(2):
                    last = mm(psOE[place % 2][:, r, :], HE[:, place % 2, r * SP_:(r + 1) * SP_], WR[:, place % RING, 2 * D:3 * D],
                              start=True, stop=True)
                last.then_inc(S["oe_done"], 1)

            def step(turn, place):
                if place + 1 < E0:
                    flip(turn, place + 1)
                gate_up(turn, place)
                if place:
                    down_slots(turn, place - 1)

            flip(0, 0)
            expert_steps(pe, step, range(PEEL), range(PEEL + 60, E0))
            down_slots(0, E0 - 1)

            def all_tokens():
                with pe.Fori(0, E0 // 2) as i:
                    for s in range(2):
                        pe.wait_ge(w_loaded[s], (i + 1) * 16)
                        W13 = WE[:, s, 0:2 * D].rearrange("p (k a c) -> p k a c", k=KC, a=2)
                        W2 = WE[:, s, 2 * D:3 * D]
                        for q in range(2):
                            pe.wait_ge(S["h_done"], (i * 2 + s) * 2 + q)
                            for a in range(2):
                                for k in range(KC):
                                    last = mm(PS[:, a, :], W13[:, k, a, :], XNT[:, k, q * 512:(q + 1) * 512],
                                              start=(k == 0), stop=(k == KC - 1))
                            last.then_inc(S["gu_done"], 1)
                            pe.wait_ge(S["h_done"], (i * 2 + s) * 2 + q + 1)
                            for t in range(4):
                                n = q * 4 + t
                                if n < 4:
                                    pe.wait_ge(S["o_used"], (i * 2 + s) * TT + (n + 1) - 1)
                                else:
                                    pe.wait_ge(S["o_used"], (i * 2 + s) * TT + n - 3)
                                mm(PS[:, 4 + t, 0:D], HH[:, q, t * P:(t + 1) * P], W2,
                                   start=True, stop=True).then_inc(S["o_done"], 1)

            pe.wait_ge(S["flag_ready"], 1)
            with pe.If(pe.value_load(FLAG[0:1, 0:1])):
                all_tokens()
            pe.wait_ge(S["loaded_l1"], 16 * 6)
            pe.wait_ge(S["oe_copied"], E0)
            pe.wait_ge(S["pool_set"], 5)
            with pe.Fori(0, B) as b:
                pe.wait_ge(S["e_xn"], b + 1)
                for k in range(KC):
                    for t in range(BT):
                        last = nc.tensor.transpose(psX3[:, k, t * P:(t + 1) * P], XN[:, t, k * P:(k + 1) * P], ident)
                last.then_inc(S["e_flip"], 1)
                pe.wait_ge(S["e_ctx"], b + 1)
                pe.wait_ge(S["e_xt"], b + 1)
                for g in range(HG):
                    for k in range(KC):
                        mm(psQ[:, g, :], WQ1[:, k, g, :], XB[:, k, :], start=(k == 0), stop=(k == KC - 1))
                pe.wait_ge(S["e_acc"], b * NF)
                for g in range(HG):
                    mm(psK[:, g, :], WKV1[:, 0, g * P:(g + 1) * P], CTB[:, :], start=True, stop=True)
                for t in range(BT):
                    last = mm(PS[:, t, :], CTB[:, t * P:(t + 1) * P], WKV1[:, 1, :], start=True, stop=True)
                last.then_inc(S["e_qkv"], 1)
                pe.wait_ge(S["e_qkv_copied"], b + 1)
                for g in range(HG):
                    if g >= 2:
                        pe.wait_ge(S["e_max"], b * HG + g - 1)
                    for j in range(GH):
                        r = slice(j * HP, (j + 1) * HP)
                        for t in range(BT):
                            dst = ps1[:, g % 2, j, t * P:t * P + (t + 1) * P]
                            mm(dst, QT[r, g, t * P:(t + 1) * P], KT[r, g, 0:(t + 1) * P], start=True, stop=False)
                            last = mm(dst[:, t * P:(t + 1) * P], identb, mask_qk, start=False, stop=True)
                    last.then_inc(S["e_s1"], 1)
                pe.wait_ge(S["e_max"], (b + 1) * HG)
                for t in range(BT):
                    last = nc.tensor.transpose(psM[:, t * P:(t + 1) * P], NM[:, t, :], ident)
                last.then_inc(S["e_flipmax"], 1)
                pe.wait_ge(S["e_mt"], b + 1)
                for g in range(HG):
                    last = mm(psA[:, g, :], sel_max[:, g, :], MT[:, :], start=True, stop=True)
                last.then_inc(S["e_sel"], 1)
                pe.wait_ge(S["e_qm"], b + 1)

                def values(u):
                    pe.wait_ge(S["e_exp"], b * UNITS + u + 1)
                    for i in range(2):
                        g, j = u // 2, u % 2 * 2 + i
                        r = slice(j * HP, (j + 1) * HP)
                        mm(psO[r, g, :], VA[:, 0, g * GH + j, :], PP[:, u % 3, i, 0:N], start=True, stop=False)
                        last = mm(psO[r, g, P:N], VA[:, 1, g * GH + j, :], PP[:, u % 3, i, N:N + P], start=False, stop=True)
                    last.then_inc(S["e_av"], 1)

                for u in range(UNITS):
                    if u >= 3:
                        pe.wait_ge(S["e_exp"], b * UNITS + u - 2)
                    for i in range(2):
                        g, j = u // 2, u % 2 * 2 + i
                        r = slice(j * HP, (j + 1) * HP)
                        dst = ps2[:, u % 3, i, :]
                        mm(dst[:, 0:N], KT[r, g, 0:P], QM[r, g, :], start=True, stop=False)
                        mm(dst[:, 0:P], identb, mask_kq, start=False, stop=True)
                        mm(dst[:, N:N + P], KT[r, g, P:N], QM[r, g, P:N], start=True, stop=False)
                        last = mm(dst[:, N:N + P], identb, mask_kq, start=False, stop=True)
                    last.then_inc(S["e_s2"], 1)
                    if u >= 2:
                        values(u - 2)
                values(UNITS - 2)
                values(UNITS - 1)
                pe.wait_ge(S["e_os"], b + 1)
                for g in range(HG):
                    last = mm(psD[:, g, :], sel_den, OS[:, g, :], start=True, stop=True)
                last.then_inc(S["e_den"], 1)
                pe.wait_ge(S["e_on"], b + 1)
                for t in range(BT):
                    for g in range(HG):
                        last = mm(psY[:, t, :], ON[:, g, t * P:(t + 1) * P], WO1[:, g, :], start=(g == 0), stop=(g == HG - 1))
                last.then_inc(S["e_y"], 1)
                pe.wait_ge(S["e_xn3"], b + 1)
                for k in range(KC):
                    for t in range(BT):
                        last = nc.tensor.transpose(psX3[:, k, t * P:(t + 1) * P], XN[:, t, k * P:(k + 1) * P], ident)
                last.then_inc(S["e_flip3"], 1)
                pe.wait_ge(S["e_xt3"], b + 1)
                for t in range(BT):
                    for k in range(KC):
                        last = mm(psG[:, t, :], XB[:, k, t * P:(t + 1) * P], GATE1[:, k, :], start=(k == 0), stop=(k == KC - 1))
                last.then_inc(S["e_gate"], 1)

                def down(c):
                    pe.wait_ge(S["e_h"], b * NF + c + 1)
                    if c >= 2:
                        pe.wait_ge(S["e_acc"], b * NF + c - 1)
                    for t in range(BT):
                        last = mm(psW[:, c % 2, t, :], H1[:, c % 2, t * P:(t + 1) * P], WD1[:, c, :], start=True, stop=True)
                    last.then_inc(S["e_down"], 1)

                for c in range(NF):
                    if c >= 2:
                        pe.wait_ge(S["e_h"], b * NF + c - 1)
                    for a in range(2):
                        for k in range(KC):
                            last = mm(psGU[:, c % 2, a, :], WGU1[:, c, k, a, :], XB[:, k, :], start=(k == 0), stop=(k == KC - 1))
                    last.then_inc(S["e_gu"], 1)
                    if c:
                        down(c - 1)
                down(NF - 1)

        @block.scalar
        def _(act):
            A = nc.scalar
            act.wait_ge(S["loaded_raw"], 16)
            A.activation(SC[:, 0:1], RAW[:, 0:1], ACT.Tanh, scale=0.5).then_inc(S["tanh_done"], 1)
            A.activation(SC[:, 1:5], RAW[:, 1:5], ACT.Tanh).then_inc(S["tanh_done"], 1)
            with act.Fori(0, B) as b:
                act.wait_ge(S["projected"], b + 1)
                A.copy(QK[:, :, :], psQK).then_inc(S["qk_copied"], 1)
                act.wait_ge(S["scores_done"], b + 1)
                act.wait_ge(S["masked"], b)
                A.mul(SIM[:, :, :], psS, SIM_SCALE).then_inc(S["sim_copied"], 1)
                act.wait_ge(S["sim_copied"], b + 1)
                A.activation(TH[:, :, :], SIM[:, :, :], ACT.Tanh, scale=0.5).then_inc(S["act_mix"], 1)
                act.wait_ge(S["act_mix"], b + 1)
                A.add(TH[:, :, :], TH[:, :, :], 1.0).then_inc(S["th_ready"], 1)
                act.wait_ge(S["xn_ready"], b + 1)
                A.copy(X1[:, ds(b * BT, BT), :], XW[:, :, :])
                A.copy(XNA[:, ds(b * BT, BT), :], XN[:, :, :]).then_inc(S["xna_ready"], 1)
                act.wait_ge(S["xn_flipped"], b + 1)
                A.copy(XNT[:, :, ds(b * N, N)], psX)
                act.wait_ge(S["logits_done"], b)
                A.copy(XB[:, :, :], psX).then_inc(S["xnt_copied"], 1)
                act.wait_ge(S["max_ready"], b + 1)
                for t in range(BT):
                    last = A.activation(EX[:, t, :], LG[:, t, :], ACT.Exp, bias=SM[:, t, 0:1], accum_out=SM[:, t, 1:2])
                last.then_inc(S["exp_done"], 1)
            A.preload_act_table(ACT.Silu)

            def copy_flipped(turn, place):
                e = turn * RING + place
                act.wait_ge(S["xt_flipped"], e + 1)
                if reused(turn, place, 2):
                    act.wait_ge(S["gue_done"], e - 1)
                A.copy(XTE[:, place % 2, :, :], psXE[place % 2]).then_inc(S["xt_copied"], 1)

            def step(turn, place):
                e = turn * RING + place
                if place + 1 < E0:
                    copy_flipped(turn, place + 1)
                act.wait_ge(S["gue_done"], e + 1)
                if reused(turn, place, 2):
                    act.wait_ge(S["he_done"], e - 1)
                A.activation(SGE[:, place % 2, :], psGE[place % 2][:, 0, :], ACT.Silu).then_inc(S["silue_done"], 1)

            copy_flipped(0, 0)
            expert_steps(act, step, range(PEEL), range(PEEL + 60, E0))

            def all_tokens():
                with act.Fori(0, E0) as e:
                    for q in range(2):
                        act.wait_ge(S["gu_done"], e * 2 + q + 1)
                        if q == 0:
                            act.wait_ge(S["h_done"], e * 2)
                        A.activation(SG[:, q, :], PS[:, 0, :], ACT.Silu).then_inc(S["silu_done"], 1)

            act.wait_ge(S["flag_ready"], 1)
            with act.If(act.value_load(FLAG[0:1, 0:1])):
                all_tokens()
            with act.Fori(0, B) as b:
                act.wait_ge(S["e_flip"], b + 1)
                A.copy(XB[:, :, :], psX3).then_inc(S["e_xt"], 1)
                act.wait_ge(S["e_qkv"], b + 1)
                A.copy(QT[:, :, :], psQ)
                A.activation(KT[:, :, :], psK, ACT.Identity, bias=k_one)
                A.copy(VA[:, :, :, 0:HD], psV[:, :, :, 0:HD]).then_inc(S["e_qkv_copied"], 1)
                act.wait_ge(S["e_flipmax"], b + 1)
                A.copy(MT[:, :], psM).then_inc(S["e_mt"], 1)
                for u in range(UNITS):
                    act.wait_ge(S["e_s2"], b * UNITS + u + 1)
                    if u >= 3:
                        act.wait_ge(S["e_av"], b * UNITS + u - 2)
                    A.activation(PP[:, u % 3, :, :], ps2[:, u % 3, :, 0:N + P], ACT.Exp, scale=HEAD_SCALE).then_inc(S["e_exp"], 1)
                act.wait_ge(S["e_av"], (b + 1) * UNITS)
                A.copy(OS[:, :, :], psO).then_inc(S["e_os"], 1)
                act.wait_ge(S["e_flip3"], b + 1)
                A.copy(XB[:, :, :], psX3).then_inc(S["e_xt3"], 1)
                act.wait_ge(S["e_gmax"], b + 1)
                for t in range(BT):
                    A.activation(EG[:, t, 0:E1], G14[:, t, 0:E1], ACT.Exp, bias=GS[:, t, 0:1])
                A.activation(EG[:, :, E1:E1 + 1], GS[:, :, 2:3], ACT.Exp, scale=-1.0)
                for t in range(BT):
                    last = A.activation(EG[:, t, E1 + 1:E1 + 2], TP[:, t, 1:2], ACT.Exp, bias=GS[:, t, 0:1])
                last.then_inc(S["e_gexp"], 1)
                for c in range(NF):
                    act.wait_ge(S["e_gu"], b * NF + c + 1)
                    if c >= 2:
                        act.wait_ge(S["e_h"], b * NF + c - 1)
                    A.activation(SG1[:, c % 2, :], psGU[:, c % 2, 0, :], ACT.Silu).then_inc(S["e_silu"], 1)

        @block.vector
        def _(dve):
            V = nc.vector
            st = Steps(dve, S["dve_scalar"])
            dve.wait_ge(S["tanh_done"], 2)
            st.done(V.tensor_scalar(SC[:, 5:6], SC[:, 0:1], 1.0, 0.125, ALU.add, ALU.mult))
            st.done(V.tensor_scalar(SC[:, 6:7], SC[:, 0:1], -0.5, 0.5, ALU.mult, ALU.add))
            st.wait()
            st.done(V.tensor_tensor(SC[:, 5:6], SC[:, 5:6], SC[:, 1:2], ALU.mult))
            st.done(V.tensor_tensor(SC[:, 6:7], SC[:, 6:7], SC[:, 1:2], ALU.mult))
            st.wait()
            V.memset(GB[:, :, :, :], 0.0).then_inc(S["zero_set"], 1)
            st.done(V.memset(MA[:, :], 0.0))
            st.wait()
            st.end()
            c_graph, c_norm = SC[:, 5:6], SC[:, 6:7]
            c_ffn0, c_att1, c_ffn1 = SC[:, 3:4], SC[:, 2:3], SC[:, 4:5]

            def norm_stats(st, src):
                for t in range(BT):
                    st.done(V.bn_stats(ST[:, t, :], src(t)))
                st.wait()
                for t in range(BT):
                    st.done(V.bn_aggr(MV[:, t, :], ST[:, t, :]))
                st.wait()
                v, y, h = RS[:, :, 3:4], RS[:, :, 0:1], RS[:, :, 4:5]
                st.done(V.tensor_scalar(v, MV[:, :, 1:2], EPS, None, ALU.add))
                st.wait()
                st.done(V.tensor_scalar(y.bitcast(I32), v.bitcast(I32), -0.5, RSQRT_GUESS, ALU.mult, ALU.add))
                for _ in range(NEWTON):
                    st.wait()
                    st.done(V.scalar_tensor_tensor(h, y, -0.5, y, ALU.mult, ALU.mult))
                    st.wait()
                    st.done(V.tensor_tensor(h, h, v, ALU.mult))
                    st.wait()
                    st.done(V.scalar_tensor_tensor(y, h, 1.5, y, ALU.add, ALU.mult))
                st.wait()

            def norm(st, src):
                norm_stats(st, lambda t: src[:, t, :])
                for t in range(BT):
                    last = V.tensor_scalar(XN[:, t, :], src[:, t, :], MV[:, t, 0:1], RS[:, t, 0:1], ALU.subtract, ALU.mult)
                return last

            dve.wait_ge(S["loaded_x"], 16)
            with dve.Fori(0, B) as b:
                st = Steps(dve, S["dve_mix"])
                norm_stats(st, lambda t: X[:, ds(b * BT + t, 1), :])
                st.done(V.tensor_scalar(RS[:, :, 1:2], RS[:, :, 0:1], c_norm, None, ALU.mult))
                st.wait()
                st.done(V.scalar_tensor_tensor(RS[:, :, 2:3], MV[:, :, 0:1], -1.0, RS[:, :, 1:2], ALU.mult, ALU.mult))
                st.wait()
                dve.wait_ge(S["sim_copied"], b + 1)
                for t in range(BT):
                    last = V.tensor_scalar(BASE[:, t, :], X[:, ds(b * BT + t, 1), :], RS[:, t, 1:2], RS[:, t, 2:3], ALU.mult, ALU.add)
                    st.done(last)
                for r in range(ROUNDS):
                    src = SIM if r == 0 else WORK
                    for t in range(BT):
                        if r:
                            st.wait(1)
                        st.done(V.max(TOP[:, t, :], src[:, t, :]))
                    if r < ROUNDS - 1:
                        for t in range(BT):
                            st.wait(1)
                            st.done(V.match_replace(WORK[:, t, :], TOP[:, t, :], src[:, t, :], LOWEST))
                st.wait()
                k = (KTH - 1) % 8
                dve.wait_ge(S["th_ready"], b + 1)
                for t in range(BT):
                    last = V.scalar_tensor_tensor(AM[:, t, :], SIM[:, t, :], TOP[:, t, k:k + 1], TH[:, t, :], ALU.is_ge, ALU.mult)
                last.then_inc(S["masked"], 1)
                dve.wait_ge(S["masked"], b + 1)
                Xb = X[:, ds(b * BT, BT), :]
                st.done(V.tensor_tensor(BASE[:, :, :], BASE[:, :, :], Xb, ALU.add))
                st.wait()
                st.done(V.scalar_tensor_tensor(XW[:, :, :], AM[:, :, :], c_graph, BASE[:, :, :], ALU.mult, ALU.add))
                st.wait()
                dve.wait_ge(S["flipped"], b + 1)
                st.done(V.scalar_tensor_tensor(XW[:, :, :], psT, c_graph, XW[:, :, :], ALU.mult, ALU.add))
                st.wait()
                norm(st, XW).then_inc(S["xn_ready"], 1)
                dve.wait_ge(S["logits_done"], b + 1)
                st.done(V.tensor_copy(LG[:, :, :], psL))
                st.wait()
                for t in range(BT):
                    st.done(V.max(L8[:, t, :], LG[:, t, :]))
                st.wait()
                V.tensor_scalar(SM[:, :, 0:1], L8[:, :, 0:1], -1.0, None, ALU.mult).then_inc(S["max_ready"], 1)
                for t in range(BT):
                    st.done(V.match_replace(LR[:, t, :], L8[:, t, :], LG[:, t, :], LOWEST))
                st.wait()
                V.tensor_tensor(MB[:, :, :], LG[:, :, :], LR[:, :, :], ALU.not_equal).then_inc(S["mask_ready"], 1)
                dve.wait_ge(S["mask_ready"], b + 1)
                dve.wait_ge(S["exp_done"], b + 1)
                st.done(V.reciprocal(SM[:, :, 2:3], SM[:, :, 1:2]))
                st.wait()
                for t in range(BT):
                    st.done(V.scalar_tensor_tensor(C0[:, ds(b * BT + t, 1), :], EX[:, t, :], SM[:, t, 2:3], MB[:, t, :], ALU.mult, ALU.mult))
                dve.wait_ge(S["ranked"], b + 1)
                st.done(V.tensor_scalar(OV[:, :, :], psR, float(CAP), None, ALU.is_ge))
                st.done(V.tensor_tensor(K1[:, :, :], psR, slot_base, ALU.add))
                st.done(V.tensor_tensor(MA[:, :], MA[:, :], MB[:, 0, :], ALU.add))
                st.wait()
                st.done(V.tensor_tensor(MA[:, :], MA[:, :], MB[:, 1, :], ALU.add))
                st.done(V.scalar_tensor_tensor(K1[:, :, :], OV[:, :, :], SKIP, K1[:, :, :], ALU.mult, ALU.add))
                st.done(V.tensor_tensor(C0X[:, ds(b * BT, BT), :], C0[:, ds(b * BT, BT), :], OV[:, :, :], ALU.mult))
                st.wait()
                st.done(V.tensor_tensor(K1[:, :, :], K1[:, :, :], MB[:, :, :], ALU.mult))
                st.done(V.tensor_tensor(C0M[:, ds(b * BT, BT), :], C0[:, ds(b * BT, BT), :], C0X[:, ds(b * BT, BT), :], ALU.subtract))
                st.wait()
                for t in range(BT):
                    st.done(V.max(KW[:, t, :], K1[:, t, :]))
                st.done(V.tensor_copy(KEY[:, ds(b * BT, BT), :], K1[:, :, :]))
                st.wait()
                st.done(V.tensor_copy(K8[:, ds(b * BT, BT), :], KW[:, :, :]))
                V.tensor_scalar(IDX[:, ds(b * BT, BT), :], KW[:, :, :], -1.0, None, ALU.add).then_inc(S["idx_ready"], 1)
                st.wait()
                st.end()
            st = Steps(dve, S["dve_w8"])
            dve.wait_ge(S["counted"], 1)
            st.done(V.tensor_reduce(FM[:, :], psN, AX.X, ALU.max))
            st.wait()
            V.tensor_scalar(FLAG[:, :], FM[:, :], float(CAP), None, ALU.is_gt).then_inc(S["flag_ready"], 1)
            for t in range(TT):
                st.wait()
                st.done(V.tensor_tensor(EQ[:, :, :], KEY[:, t:t + 1, :].to_broadcast([P, TOP0, E0]),
                                        K8[:, t, :].unsqueeze(2).to_broadcast([P, TOP0, E0]), ALU.is_equal))
                st.wait()
                st.done(V.tensor_tensor(EQ[:, :, :], EQ[:, :, :], C0M[:, t:t + 1, :].to_broadcast([P, TOP0, E0]), ALU.mult))
                st.wait()
                st.done(V.tensor_reduce(W8[:, t, :], EQ[:, :, :], AX.X, ALU.add))
            st.end()

            def copy_out(turn, place):
                e = turn * RING + place
                dve.wait_ge(S["oe_done"], e + 1)
                if reused(turn, place, 3):
                    dve.wait_ge(oe_stored[place % 3], uses(turn, place, 3) * 16)
                V.tensor_copy(OE[:, place % 3, :, :], psOE[place % 2]).then_inc(S["oe_copied"], 1)

            def step(turn, place):
                e = turn * RING + place
                dve.wait_ge(S["silue_done"], e + 1)
                if reused(turn, place, 2):
                    dve.wait_ge(S["oe_done"], e - 1)
                V.tensor_tensor(HE[:, place % 2, :], SGE[:, place % 2, :], psGE[place % 2][:, 1, :], ALU.mult).then_inc(S["he_done"], 1)
                if place:
                    copy_out(turn, place - 1)

            expert_steps(dve, step, range(PEEL), range(PEEL + 60, E0))
            copy_out(0, E0 - 1)

            def all_tokens():
                dve.wait_ge(S["pool_set"], 5)
                with dve.Fori(0, E0) as e:
                    for q in range(2):
                        dve.wait_ge(S["silu_done"], e * 2 + q + 1)
                        if q == 0:
                            dve.wait_ge(S["o_done"], e * TT)
                        V.tensor_tensor(HH[:, q, :], SG[:, q, :], PS[:, 1, :], ALU.mult).then_inc(S["h_done"], 1)
                        for t in range(4):
                            n = q * 4 + t
                            dve.wait_ge(S["o_done"], e * TT + n + 1)
                            V.scalar_tensor_tensor(MOE[:, n, :], PS[:, 4 + t, 0:D], C0X[:, n, ds(e, 1)], MOE[:, n, :],
                                                   ALU.mult, ALU.add).then_inc(S["o_used"], 1)

                dve.wait_ge(S["o_used"], E0 * TT)

            with dve.If(dve.value_load(FLAG[0:1, 0:1])):
                all_tokens()
            dve.sem_inc(S["general_done"], 1)
            dve.wait_ge(S["pool_set"], 5)
            with dve.Fori(0, B) as b:
                st = Steps(dve, S["dve_l1"])
                for t in range(BT):
                    dve.wait_ge(gathered[t], (b + 1) * (16 * TOP0))
                    for j in range(TOP0):
                        if j:
                            st.wait()
                        so_far = X2[:, t, :] if j else MOE[:, ds(b * BT + t, 1), :]
                        last = V.scalar_tensor_tensor(X2[:, t, :], GB[:, t, j, :], W8[:, ds(b * BT + t, 1), j:j + 1], so_far, ALU.mult, ALU.add)
                        if j < TOP0 - 1:
                            st.done(last)
                    last.then_inc(S["gb_used"], 1)
                dve.wait_ge(S["gb_used"], b * BT + BT)
                st.done(V.scalar_tensor_tensor(X2[:, :, :], X2[:, :, :], c_ffn0, X1[:, ds(b * BT, BT), :], ALU.mult, ALU.add))
                st.wait()
                norm(st, X2).then_inc(S["e_xn"], 1)
                for g in range(HG):
                    dve.wait_ge(S["e_s1"], b * HG + g + 1)
                    for t in range(BT):
                        last = V.tensor_reduce(NM[:, t, g * GH:(g + 1) * GH], ps1[:, g % 2, :, t * P:t * P + (t + 1) * P],
                                               AX.X, ALU.max, negate=True)
                    last.then_inc(S["e_max"], 1)
                dve.wait_ge(S["e_sel"], b + 1)
                V.tensor_tensor(QM[:, :, :], psA, QT[:, :, :], ALU.add).then_inc(S["e_qm"], 1)
                dve.wait_ge(S["e_den"], b + 1)
                st.done(V.reciprocal(RD[:, :, :], psD))
                st.wait()
                V.tensor_tensor(ON[:, :, :], OS[:, :, :], RD[:, :, :], ALU.mult).then_inc(S["e_on"], 1)
                dve.wait_ge(S["e_y"], b + 1)
                st.done(V.scalar_tensor_tensor(X3[:, :, :], psY, c_att1, X2[:, :, :], ALU.mult, ALU.add))
                st.wait()
                norm(st, X3).then_inc(S["e_xn3"], 1)
                dve.wait_ge(S["e_gate"], b + 1)
                st.done(V.tensor_copy(G14[:, :, 0:E1], psG[:, :, 0:E1]))
                st.done(V.tensor_copy(GS[:, :, 2:3], psG[:, :, E1:E1 + 1]))
                st.wait()
                for t in range(BT):
                    st.done(V.max(T8[:, t, :], G14[:, t, 0:E1]))
                st.wait()
                st.done(V.tensor_copy(TP[:, :, 0:2], T8[:, :, 0:2]))
                st.done(V.tensor_scalar(GS[:, :, 0:1], T8[:, :, 0:1], -1.0, None, ALU.mult))
                st.wait()
                V.tensor_scalar(GS[:, :, 1:2], T8[:, :, 0:1], 1.0, None, ALU.mult).then_inc(S["e_gmax"], 1)
                for t in range(BT):
                    st.done(V.match_replace(G14R[:, t, 0:14], TP[:, t, :], G14[:, t, 0:14], LOWEST))
                st.wait()
                st.done(V.tensor_tensor(G14R[:, :, 0:E1], G14[:, :, 0:E1], G14R[:, :, 0:E1], ALU.not_equal))
                dve.wait_ge(S["e_gexp"], b + 1)
                st.done(V.tensor_scalar(EG[:, :, E1:E1 + 2], EG[:, :, E1:E1 + 2], 1.0, None, ALU.add))
                st.wait()
                st.done(V.reciprocal(EG[:, :, E1 + 2:E1 + 4], EG[:, :, E1:E1 + 2]))
                st.wait()
                st.done(V.tensor_copy(CM[:, :, E1:E1 + 1], EG[:, :, E1 + 2:E1 + 3]))
                for t in range(BT):
                    st.done(V.scalar_tensor_tensor(CM[:, t, 0:E1], EG[:, t, 0:E1], EG[:, t, E1 + 3:E1 + 4], G14R[:, t, 0:E1],
                                                   ALU.mult, ALU.mult))
                st.wait()

                def add_up(c):
                    dve.wait_ge(S["e_down"], b * NF + c + 1)
                    for t in range(BT):
                        w = CM[:, t, min(c, E1):min(c, E1) + 1]
                        if c == 0:
                            last = V.tensor_scalar(FA[:, t, :], psW[:, c % 2, t, :], w, None, ALU.mult)
                        else:
                            last = V.scalar_tensor_tensor(FA[:, t, :], psW[:, c % 2, t, :], w, FA[:, t, :], ALU.mult, ALU.add)
                    last.then_inc(S["e_acc"], 1)

                for c in range(NF):
                    dve.wait_ge(S["e_silu"], b * NF + c + 1)
                    if c >= 2:
                        dve.wait_ge(S["e_down"], b * NF + c - 1)
                    V.tensor_tensor(H1[:, c % 2, :], SG1[:, c % 2, :], psGU[:, c % 2, 1, :], ALU.mult).then_inc(S["e_h"], 1)
                    if c:
                        if c > 1:
                            dve.wait_ge(S["e_acc"], b * NF + c - 1)
                        add_up(c - 1)
                dve.wait_ge(S["e_acc"], b * NF + NF - 1)
                add_up(NF - 1)
                dve.wait_ge(S["e_acc"], (b + 1) * NF)
                dve.wait_ge(S["stored"], b * 16)
                V.scalar_tensor_tensor(OUT[:, :, :], FA[:, :, :], c_ffn1, X3[:, :, :], ALU.mult, ALU.add).then_inc(S["e_out"], 1)
                st.end()


def kernel(**inputs):
    import ml_dtypes
    import numpy as np
    import concourse.bacc as bacc
    from concourse.bass_utils import run_bass_kernel_spmd

    def at(name):
        return np.asarray(inputs[name])

    def pad_heads(w):
        k = w.shape[0]
        padded = np.zeros((k, NH, HP), w.dtype)
        padded[:, :, :HD] = w.reshape(k, NH, HD)
        return padded.reshape(k, NH * HP)

    def chunks(w):
        return w.reshape(-1, P, w.shape[-1]).transpose(1, 0, 2)

    w13, w2 = at("L0_ffn_w13"), at("L0_ffn_w2")
    w13T = w13.transpose(0, 2, 1).reshape(E0, KC, P, 2 * I0).transpose(0, 2, 1, 3).reshape(E0, P, KC * 2 * I0)
    wexp = np.concatenate([w13T, w2.transpose(0, 2, 1)], axis=2).reshape(E0 * P, 3 * D)
    wkv = at("L1_xattn_Wkv_expand").T
    gate = np.concatenate([at("L1_ffn_w_gate"), at("L1_ffn_sh_gate").reshape(2, P, D)])
    up = np.concatenate([at("L1_ffn_w_up"), at("L1_ffn_sh_up").reshape(2, P, D)])
    gu = np.stack([gate, up], axis=1)
    wgu = gu.reshape(NF, 2, P, KC, P).transpose(4, 0, 3, 1, 2)
    down = np.concatenate([at("L1_ffn_w_down").transpose(0, 2, 1), at("L1_ffn_sh_down").T.reshape(2, P, D)])
    raw = np.concatenate([at("L0_xattn_gamma_raw").reshape(1), at("g_xattn"), at("g_ffn")])[None, :]

    row, col = np.arange(P)[:, None], np.arange(P)[None, :]
    cf = np.zeros((P, 2 * P + HG * P + 1 + BT * E0), np.float32)
    cf[:, 0:P] = np.eye(P)
    cf[:, P:2 * P] = row == col // HP * HP + HD
    for h in range(NH):
        cf[h, 2 * P + h * HP + HD] = 1.0
    cf[:, 2 * P + HG * P] = np.arange(P) % HP == HD
    cf[:, 2 * P + HG * P + 1:] = np.tile(np.arange(E0) * CAP + 1, BT)
    cb = np.zeros((P, 5, P), ml_dtypes.bfloat16)
    cb[:, 0] = np.eye(P)
    cb[:, 1] = np.where(col > row, -1.0e38, 0.0)
    cb[:, 2] = np.where(row > col, -1.0e38, 0.0)
    cb[:, 3] = row < col
    cb[:, 4] = 1.0

    ins = {
        "x": at("x").reshape(T, D),
        "ctxT": at("ctx_512").reshape(T, DC).T,
        "raw": raw,
        "wqk0": np.pad(np.stack([at("L0_xattn_Wq").T, at("L0_xattn_Wk").T], axis=1), ((0, 0), (0, 0), (0, P - DC))),
        "gate0": chunks(at("L0_ffn_gate_w").T),
        "wexp": wexp,
        "wq1": chunks(pad_heads(at("L1_xattn_Wq").T)).reshape(P, KC, HG, P),
        "wkv1": np.stack([pad_heads(wkv[:, :D]), pad_heads(wkv[:, D:])], axis=1),
        "wo1": pad_heads(at("L1_xattn_Wout")).T.reshape(HG, P, D).transpose(1, 0, 2),
        "gate1": chunks(np.concatenate([at("L1_ffn_gate_w"), at("L1_ffn_se_gate_w")]).T),
        "wgu1": wgu,
        "wd1": down.transpose(1, 0, 2),
        "cf": cf,
        "cb": cb,
    }
    nc = bacc.Bacc("TRN2", target_bir_lowering=False, num_devices=1)
    arrays, args = {}, []
    for name, a in ins.items():
        a = np.ascontiguousarray(a)
        arrays[f"in_{name}"] = a
        args.append(nc.dram_tensor(f"in_{name}", a.shape, mybir.dt.from_np(a.dtype), kind="ExternalInput").ap())
    args.append(nc.dram_tensor("out_0", (T, D), F32, kind="ExternalOutput").ap())
    xs = nc.dram_tensor("slots_in", (SLOTS, D), F32, kind="Internal").ap()
    ys = nc.dram_tensor("slots_out", (SLOTS, D), F32, kind="Internal").ap()
    gated_block(nc, xs, ys, *args)
    r = run_bass_kernel_spmd(nc, [arrays], core_ids=[0])
    return r.results[0]["out_0"].reshape(B, N, D)
```

```python
from contextlib import ExitStack

import concourse.bass as bass
from concourse import mybir

F32 = mybir.dt.float32
BF16 = mybir.dt.bfloat16
I32 = mybir.dt.int32
F32R = mybir.dt.float32r
ACT = mybir.ActivationFunctionType
ALU = mybir.AluOpType
AX = mybir.AxisListType
ds = bass.ds

P = 128
B, N, D = 4, 256, 256
DC = 64
T = B * N
TT = T // P
BT = N // P
KC = D // P
E0, TOP0 = 64, 8
I0 = 128
CAP = 192
SP_ = CAP // 2
SLOTS = E0 * CAP
SKIP = 65536.0
RING = 12
XRING = 4
PEEL = 3
KTH = int(N * 0.3)
ROUNDS = (KTH + 7) // 8
NH, HD = 16, 16
HP = 32
HG, GH = NH * HP // P, P // HP
HS = 64
UNITS = NH * HS // P
E1 = 8
NF = E1 + 2
EPS = 1e-5
RSQRT_GUESS = float(0x5F3759DF)
NEWTON = 3
LOWEST = -3.0e38
SIM_SCALE = 1.0 / 16.0
HEAD_SCALE = HD ** -0.5


class Steps:

    def __init__(self, eng, sem):
        self.eng, self.sem, self.n = eng, sem, 0

    def done(self, ins):
        self.n += 1
        ins.then_inc(self.sem, 1)

    def wait(self, behind=0):
        self.eng.wait_ge(self.sem, self.n - behind)

    def end(self):
        self.wait()
        self.eng.sem_clear(self.sem)
        self.n = 0


def gated_block(nc, xs, ys, x, ctxT, raw, wqk0, gate0, wexp, wq1, wk1, wv1, wo1, gate1, wgu1, wd1, spread, cf, cb, out):
    with ExitStack() as ctx:
        def sb(name, shape, dt=F32):
            return ctx.enter_context(nc.sbuf_tensor(name, shape, dt))

        def sem(name):
            return ctx.enter_context(nc.semaphore(name))

        X = sb("X", [P, TT, D])
        CT = sb("CT", [DC, T])
        WQK0 = sb("WQK0", [DC, 2, P])
        GATE0 = sb("GATE0", [P, KC, E0])
        WQ1 = sb("WQ1", [P, KC, KC, P])
        WK1 = sb("WK1", [DC, KC, P])
        WV1 = sb("WV1", [DC, D])
        WO1 = sb("WO1", [P, KC, D])
        GATE1 = sb("GATE1", [P, KC, E1 + 1])
        with ExitStack() as early:
            WGU1 = early.enter_context(nc.sbuf_tensor("WGU1", [P, NF, KC, 2, P], F32))
        QS = sb("QS", [P, UNITS, 2, N], F32R)
        XH = sb("XH", [P, KC, N], F32R)
        XL = sb("XL", [P, KC, N], F32R)
        WD1 = sb("WD1", [P, NF, D])
        SPREADB = sb("SPREADB", [P, 4, UNITS // KC, P], BF16)
        CF = sb("CF", [P, P + NH + BT * E0])
        ident, sel_head = CF[:, 0:P], CF[:, P:P + NH]
        slot_base = CF[:, P + NH:].rearrange("p (t e) -> p t e", t=BT)
        CB = sb("CB", [P, 5, P], BF16)
        identb, mask_qk, mask_kq, before, onesb = (CB[:, i, :] for i in range(5))
        RAW = sb("RAW", [P, 5])
        SC = sb("SC", [P, 8])
        X1 = sb("X1", [P, TT, D])
        MOE = sb("MOE", [P, TT, D])
        K8 = sb("K8", [P, TT, TOP0])
        IDX = sb("IDX", [P, TT, TOP0], I32)
        W8 = sb("W8", [P, TT, TOP0])
        with ExitStack() as early:
            def sb_early(name, shape):
                return early.enter_context(nc.sbuf_tensor(name, shape, F32))

            XNT = sb_early("XNT", [P, KC, T])
            XNA = sb_early("XNA", [P, TT, D])
            C0 = sb_early("C0", [P, TT, E0])
            KEY = sb_early("KEY", [P, TT, E0])
            C0M = sb_early("C0M", [P, TT, E0])
            C0X = sb_early("C0X", [P, TT, E0])
            WR = sb_early("WR", [P, RING, 3 * D])
            XE = sb_early("XE", [SP_, XRING, 2, D])
            XTE = sb_early("XTE", [P, 2, KC, CAP])
            SGE = sb_early("SGE", [P, 2, CAP])
            HE = sb_early("HE", [P, 2, CAP])
            OE = sb_early("OE", [SP_, 3, 2, D])
        KP = sb("KP", [P, 2, KC, N], F32R)
        QP = sb("QP", [P, 2, KC, N], F32R)
        SPREAD = sb("SPREAD", [P, 4, UNITS // KC, P], F32R)
        SEL = sb("SEL", [P, NH, P], F32R)
        KS = sb("KS", [P, UNITS, N], F32R)
        PP = sb("PP", [P, 2 * GH, N + P])
        WGH = sb("WGH", [P, NF, KC, 2, P], F32R)
        WGL = sb("WGL", [P, NF, KC, 2, P], F32R)
        XB3 = sb("XB3", [P, KC * N])
        QK = sb("QK", [P, 2, N])
        SIM = sb("SIM", [P, BT, N])
        TH = sb("TH", [P, BT, N])
        WORK = sb("WORK", [P, BT, N])
        TOP = sb("TOP", [P, BT, 8])
        AM = sb("AM", [P, BT, N])
        BASE = sb("BASE", [P, BT, N])
        XW = sb("XW", [P, BT, D])
        XN = sb("XN", [P, BT, D])
        ST = sb("ST", [P, BT, 6])
        MV = sb("MV", [P, BT, 2])
        RS = sb("RS", [P, BT, 8])
        STX = sb("STX", [P, TT, 6])
        MVX = sb("MVX", [P, TT, 2])
        RSX = sb("RSX", [P, TT, 8])
        XB = sb("XB", [P, KC, N])
        LG = sb("LG", [P, BT, E0])
        LR = sb("LR", [P, BT, E0])
        MB = sb("MB", [P, BT, E0], BF16)
        MA = sb("MA", [P, E0], BF16)
        OV = sb("OV", [P, BT, E0])
        K1 = sb("K1", [P, BT, E0])
        KW = sb("KW", [P, BT, 8])
        FM = sb("FM", [P, 1])
        FLAG = sb("FLAG", [P, 1], I32)
        EQ = sb("EQ", [P, TOP0, E0])
        EX = sb("EX", [P, BT, E0])
        L8 = sb("L8", [P, BT, 8])
        SM = sb("SM", [P, BT, 4])
        GB = sb("GB", [P, BT, TOP0, D])
        WE = WR
        ZERO = GB[:, 0, :, :].rearrange("p j d -> p (j d)")
        SG = GB[:, 0, 0:4, :].rearrange("p (q k) n -> p q (k n)", q=2)
        HH = GB[:, 0, 4:8, :].rearrange("p (q k) n -> p q (k n)", q=2)
        CTB = sb("CTB", [DC, N])
        X2, X3, FA, OUT, SG1, H1, XR = BASE, SIM, TH, WORK, AM, XW, QK
        XN3 = EQ.rearrange("p j e -> p (j e)").rearrange("p (t d) -> p t d", t=BT)
        XF = X[:, :, :].rearrange("p t d -> p (t d)")
        OS = XF[:, 0:HG * N].rearrange("p (g n) -> p g n", g=HG)
        ONT = XF[:, HG * N:HG * N + BT * D].rearrange("p (t d) -> p t d", t=BT)
        ON = XF[:, HG * N + BT * D:].rearrange("p (k n) -> p k n", k=KC)
        VA = sb("VA", [P, BT, NH, HP])
        NM = sb("NM", [P, BT, NH])
        NMP = sb("NMP", [P, BT, 2, NH], F32R)
        MT = sb("MT", [P, N], F32R)
        RD = sb("RD", [P, BT, NH])
        G14 = sb("G14", [P, BT, 16])
        G14R = sb("G14R", [P, BT, 16])
        TP = sb("TP", [P, BT, 8])
        T8 = sb("T8", [P, BT, 8])
        EG = sb("EG", [P, BT, 16])
        ZP = sb("ZP", [P, 1])
        CM = sb("CM", [P, BT, E1 + 1])
        GS = sb("GS", [P, BT, 8])

        PS = ctx.enter_context(nc.psum_tensor("PS", [P, 8, 512], F32))

        psQK = PS[:, 0, :].rearrange("p (a n) -> p a n", a=2)
        psS = PS[:, 1, :].rearrange("p (a n) -> p a n", a=2)
        psT = PS[:, 2, :].rearrange("p (a n) -> p a n", a=2)
        psX = PS[:, 3, :].rearrange("p (a n) -> p a n", a=2)
        psL = PS[:, 4, 0:BT * E0].rearrange("p (a n) -> p a n", a=BT)
        psR = PS[:, 5, 0:BT * E0].rearrange("p (a n) -> p a n", a=BT)
        psN = PS[:, 6, 0:E0]
        psXE = [PS[:, i, 0:KC * CAP].rearrange("p (k n) -> p k n", k=KC) for i in range(2)]
        psGE = [PS[:, 2 + i, 0:2 * CAP].rearrange("p (a n) -> p a n", a=2) for i in range(2)]
        psOE = [PS[0:SP_, 4 + i, :].rearrange("p (r n) -> p r n", r=2) for i in range(2)]
        psKc = PS[:, 3, :].rearrange("p (a n) -> p a n", a=2)
        psQc = PS[:, 4, :].rearrange("p (a n) -> p a n", a=2)
        psK = PS[:, 0:4, :].rearrange("p b (g n) -> p (b g) n", g=2)
        psQ = psK
        ps1 = PS[:, 0:4, :].rearrange("p (s h) c -> p s h c", s=2)
        psM = PS[0:2 * NH, 0, 0:N]
        ps2 = PS[:, 0:3, :]
        psO = PS[:, 3:5, :].rearrange("p b (g n) -> p (b g) n", g=2)
        psOT = PS[:, 0:2, :].rearrange("p t (h c) -> p t h c", h=NH)
        psNT = PS[:, 2, :].rearrange("p (a n) -> p a n", a=2)
        psY = psV = psX2 = psX3 = PS[:, 4, :].rearrange("p (a n) -> p a n", a=2)
        psG = PS[:, 4, 0:BT * (E1 + 1)].rearrange("p (a n) -> p a n", a=BT)
        psGU = PS[:, 5:7, :].rearrange("p s (a n) -> p s a n", a=2)
        psW = PS[:, 7, :].rearrange("p (a n) -> p a n", a=2)

        names = """loaded_ctx loaded_x loaded_raw loaded_gate0 loaded_l1 tanh_done projected qk_copied scores_done
            sim_copied th_ready masked flipped xn_ready xn_flipped xnt_copied logits_done max_ready exp_done
            dve_scalar dve_mix act_mix gu_done silu_done h_done o_done o_used zero_set zeroed mask_ready
            ranked xna_ready idx_ready scattered counted flag_ready all_stored general_done gb_used
            xt_flipped xt_copied gue_done silue_done he_done oe_done oe_copied dve_w8 e_ctx e_spread e_wh
            e_wl e_zeros e_xh e_xl e_va e_xr e_x3 e_xn e_flip e_xt e_k e_v e_q e_hi_k e_hi_q e_lo_k e_lo_q
            e_k_spread e_q_spread e_ks e_qs e_s1 e_max e_nm e_flipmax e_mt e_set e_s2 e_exp e_av e_os e_ot
            e_ont e_nt e_on e_y e_xn3 e_flip3 e_xt3 e_gate e_gmax e_gexp e_gu e_silu e_h e_down e_acc e_out
            dve_l1 pool_set stored""".split()
        S = {n: sem(n) for n in names}
        w_loaded = [sem(f"w_loaded{i}") for i in range(2)]
        wr_loaded = [sem(f"wr_loaded{i}") for i in range(RING)]
        xe_loaded = [sem(f"xe_loaded{i}") for i in range(XRING)]
        oe_stored = [sem(f"oe_stored{i}") for i in range(3)]
        gathered = [sem(f"gathered{i}") for i in range(BT)]

        def expert_steps(eng, step, first, last):
            for e in first:
                step(0, e)
            with eng.Fori(0, (E0 - 4) // RING) as turn:
                for u in range(RING):
                    step(turn, PEEL + u)
            for e in last:
                step(0, e)

        def uses(turn, place, ring):
            return turn * (RING // ring) + place // ring

        def reused(turn, place, ring):
            return place >= ring or not isinstance(turn, int)

        block = ctx.enter_context(nc.Block())

        @block.sync
        def _(sp):
            sp.dma_start(RAW[:, :], raw.to_broadcast([P, 5])).then_inc(S["loaded_raw"], 16)
            sp.dma_start(CT[:, :], ctxT).then_inc(S["loaded_ctx"], 16)
            sp.dma_start(WQK0[:, :, :], wqk0).then_inc(S["loaded_ctx"], 16)
            sp.dma_start(X[:, :, :], x.rearrange("(t p) d -> p t d", p=P)).then_inc(S["loaded_x"], 16)
            sp.dma_start(CF[:, :], cf).then_inc(S["loaded_gate0"], 16)
            sp.dma_start(GATE0[:, :, :], gate0).then_inc(S["loaded_gate0"], 16)
            sp.dma_start(CB[:, :, :], cb).then_inc(S["loaded_gate0"], 16)
            sp.wait_ge(S["zero_set"], 1)
            for i in range(SLOTS // (8 * P)):
                sp.dma_start(xs[i * 8 * P:(i + 1) * 8 * P, :].rearrange("(p r) d -> p (r d)", p=P), ZERO)\
                  .then_inc(S["zeroed"], 16)
            for dst, src in ((WQ1[:, :, :, :], wq1), (WK1[:, :, :], wk1), (WV1[:, :], wv1), (WO1[:, :, :], wo1),
                             (GATE1[:, :, :], gate1), (SPREADB[:, :, :, :], spread), (WGU1[:, :, :, :, :], wgu1), (WD1[:, :, :], wd1)):
                sp.dma_start(dst, src).then_inc(S["loaded_l1"], 16)
            for i in range(RING):
                sp.dma_start(WR[:, i, :], wexp[i * P:(i + 1) * P, :]).then_inc(wr_loaded[i], 16)

            def load_slots(turn, place):
                e = turn * RING + place
                sp.dma_start(XE[:, place % XRING, :, :], xs[ds(e * CAP, CAP), :].rearrange("(p r) d -> p r d", r=2))\
                  .then_inc(xe_loaded[place % XRING], 16)

            sp.wait_ge(S["scattered"], 16 * TT * TOP0)
            for e in range(XRING):
                load_slots(0, e)

            def step(turn, place):
                e = turn * RING + place
                fixed = isinstance(turn, int)
                if not fixed or e - 1 + XRING < E0:
                    sp.wait_ge(S["xt_flipped"], e)
                    load_slots(turn, place - 1 + XRING)
                if not fixed or 0 <= e - 2 < E0 - RING:
                    sp.wait_ge(S["oe_done"], e - 1)
                    sp.dma_start(WR[:, (place - 2) % RING, :], wexp[ds((e + (RING - 2)) * P, P), :])\
                      .then_inc(wr_loaded[(place - 2) % RING], 16)

            for e in range(1, PEEL):
                step(0, e)
            with sp.Fori(0, 4) as turn:
                for u in range(RING):
                    step(turn, PEEL + u)
            for e in range(PEEL + 4 * RING, E0):
                step(0, e)
            for i in range(3):
                sp.wait_ge(oe_stored[i], 16 * len(range(i, E0, 3)))
            sp.sem_inc(S["all_stored"], 1)
            sp.wait_ge(S["flag_ready"], 1)
            with sp.If(sp.value_load(FLAG[0:1, 0:1])):
                sp.wait_ge(S["he_done"], E0)
                for s in range(2):
                    sp.dma_start(WE[:, s, :], wexp[s * P:(s + 1) * P, :]).then_inc(w_loaded[s], 16)
                with sp.Fori(1, E0 // 2) as i:
                    for s in range(2):
                        sp.wait_ge(S["o_done"], (i * 2 + s - 1) * TT)
                        sp.dma_start(WE[:, s, :], wexp[ds(i * (2 * P) + s * P, P), :]).then_inc(w_loaded[s], 16)
            with sp.Fori(0, B) as b:
                sp.wait_ge(S["e_out"], b + 1)
                sp.dma_start(out[ds(b * N, N), :].rearrange("(t p) d -> p t d", p=P), OUT[:, :, :]).then_inc(S["stored"], 16)
            sp.wait_ge(S["stored"], 16 * B)

        @block.gpsimd
        def _(pool):
            nc.gpsimd.memset(GB[:, :, :, :], 0.0).then_inc(S["zero_set"], 1)
            nc.gpsimd.memset(VA[:, :, :, :], 0.0).then_inc(S["pool_set"], 1)
            pool.wait_ge(S["pool_set"], 1)
            nc.gpsimd.memset(VA[:, :, :, HD:HD + 1], 1.0).then_inc(S["pool_set"], 1)
            nc.gpsimd.memset(MOE[:, :, :], 0.0).then_inc(S["pool_set"], 1)
            nc.gpsimd.memset(G14[:, :, :], 1.0e30).then_inc(S["pool_set"], 1)
            nc.gpsimd.memset(TP[:, :, :], 1.0e30).then_inc(S["pool_set"], 1)
            pool.wait_ge(S["zeroed"], 16 * (SLOTS // (8 * P)))
            for t in range(TT):
                pool.wait_ge(S["xna_ready"], t // BT + 1)
                pool.wait_ge(S["idx_ready"], t // BT + 1)
                for j in range(TOP0):
                    pool.indirect_dma_start(out=xs, out_offset=bass.IndirectOffsetOnAxis(ap=IDX[:, t, j:j + 1], axis=0),
                                            in_=XNA[:, t, :], in_offset=None, bounds_check=SLOTS - 1, oob_is_err=False)\
                        .then_inc(S["scattered"], 16)
            pool.wait_ge(S["pool_set"], 5)
            nc.gpsimd.tensor_copy(CTB[:, :], CT[:, 0:N]).then_inc(S["e_ctx"], 1)
            pool.wait_ge(S["all_stored"], 1)
            pool.wait_ge(S["general_done"], 1)

            def gather(t):
                for j in range(TOP0):
                    pool.indirect_dma_start(out=GB[:, t % BT, j, :], out_offset=None, in_=ys,
                                            in_offset=bass.IndirectOffsetOnAxis(ap=IDX[:, t, j:j + 1], axis=0),
                                            bounds_check=SLOTS - 1, oob_is_err=False).then_inc(gathered[t % BT], 16)

            for b in range(B):
                for i in range(BT):
                    if b:
                        pool.wait_ge(S["gb_used"], b * BT + i - BT + 1)
                    gather(b * BT + i)
                if b:
                    pool.wait_ge(S["e_v"], b)
                    nc.gpsimd.tensor_copy(CTB[:, :], CT[:, b * N:(b + 1) * N]).then_inc(S["e_ctx"], 1)

        @block.tensor
        def _(pe):
            mm = nc.tensor.matmul
            pe.wait_ge(S["loaded_ctx"], 32)

            def scores(b):
                pe.wait_ge(S["qk_copied"], b)
                for a in range(2):
                    last = mm(psQK[:, a, :], WQK0[:, a, :], CT[:, ds(b * N, N)], start=True, stop=True)
                last.then_inc(S["projected"], 1)
                pe.wait_ge(S["qk_copied"], b + 1)
                pe.wait_ge(S["sim_copied"], b)
                for t in range(BT):
                    last = mm(psS[:, t, :], QK[:, 0, t * P:(t + 1) * P], QK[:, 1, :], start=True, stop=True)
                last.then_inc(S["scores_done"], 1)

            def mix(b):
                pe.wait_ge(S["masked"], b + 1)
                for t in range(BT):
                    for c in range(BT):
                        last = nc.tensor.transpose(psT[:, t, c * P:(c + 1) * P], AM[:, c, t * P:(t + 1) * P], ident)
                last.then_inc(S["flipped"], 1)

            def route(b):
                pe.wait_ge(S["xn_ready"], b + 1)
                for k in range(KC):
                    for t in range(BT):
                        last = nc.tensor.transpose(psX[:, k, t * P:(t + 1) * P], XN[:, t, k * P:(k + 1) * P], ident)
                last.then_inc(S["xn_flipped"], 1)
                pe.wait_ge(S["xnt_copied"], b + 1)
                for t in range(BT):
                    for k in range(KC):
                        last = mm(psL[:, t, :], XB[:, k, t * P:(t + 1) * P], GATE0[:, k, :], start=(k == 0), stop=(k == KC - 1))
                last.then_inc(S["logits_done"], 1)
                pe.wait_ge(S["mask_ready"], b + 1)
                for t in range(BT):
                    mm(psR[:, t, :], before, MB[:, t, :], start=True, stop=False)
                    if t:
                        mm(psR[:, t, :], onesb, MB[:, 0, :], start=False, stop=False)
                    last = mm(psR[:, t, :], onesb, MA[:, :], start=False, stop=True)
                last.then_inc(S["ranked"], 1)
            scores(0)
            pe.wait_ge(S["loaded_gate0"], 48)
            with pe.Fori(0, B - 1) as b:
                mix(b)
                scores(b + 1)
                route(b)
            mix(B - 1)
            route(B - 1)
            pe.wait_ge(S["idx_ready"], B)
            mm(psN, onesb, MA[:, :], start=True, stop=True).then_inc(S["counted"], 1)

            def flip(turn, place):
                e = turn * RING + place
                pe.wait_ge(xe_loaded[place % XRING], uses(turn, place, XRING) * 16 + 16)
                if reused(turn, place, 2):
                    pe.wait_ge(S["xt_copied"], e - 1)
                for k in range(KC):
                    for r in range(2):
                        last = nc.tensor.transpose(psXE[place % 2][:, k, r * SP_:(r + 1) * SP_],
                                                   XE[:, place % XRING, r, k * P:(k + 1) * P], ident[0:SP_, 0:SP_])
                last.then_inc(S["xt_flipped"], 1)

            def gate_up(turn, place):
                e = turn * RING + place
                pe.wait_ge(S["xt_copied"], e + 1)
                pe.wait_ge(wr_loaded[place % RING], uses(turn, place, RING) * 16 + 16)
                if reused(turn, place, 2):
                    pe.wait_ge(S["he_done"], e - 1)
                W13 = WR[:, place % RING, 0:2 * D].rearrange("p (k a c) -> p k a c", k=KC, a=2)
                for a in range(2):
                    for k in range(KC):
                        last = mm(psGE[place % 2][:, a, :], W13[:, k, a, :], XTE[:, place % 2, k, :], start=(k == 0), stop=(k == KC - 1))
                last.then_inc(S["gue_done"], 1)

            def down_slots(turn, place):
                e = turn * RING + place
                pe.wait_ge(S["he_done"], e + 1)
                if reused(turn, place, 2):
                    pe.wait_ge(S["oe_copied"], e - 1)
                for r in range(2):
                    last = mm(psOE[place % 2][:, r, :], HE[:, place % 2, r * SP_:(r + 1) * SP_], WR[:, place % RING, 2 * D:3 * D],
                              start=True, stop=True)
                last.then_inc(S["oe_done"], 1)

            def step(turn, place):
                if place + 1 < E0:
                    flip(turn, place + 1)
                gate_up(turn, place)
                if place:
                    down_slots(turn, place - 1)

            flip(0, 0)
            expert_steps(pe, step, range(PEEL), range(PEEL + 60, E0))
            down_slots(0, E0 - 1)

            def all_tokens():
                with pe.Fori(0, E0 // 2) as i:
                    for s in range(2):
                        pe.wait_ge(w_loaded[s], (i + 1) * 16)
                        W13 = WE[:, s, 0:2 * D].rearrange("p (k a c) -> p k a c", k=KC, a=2)
                        W2 = WE[:, s, 2 * D:3 * D]
                        for q in range(2):
                            pe.wait_ge(S["h_done"], (i * 2 + s) * 2 + q)
                            for a in range(2):
                                for k in range(KC):
                                    last = mm(PS[:, a, :], W13[:, k, a, :], XNT[:, k, q * 512:(q + 1) * 512],
                                              start=(k == 0), stop=(k == KC - 1))
                            last.then_inc(S["gu_done"], 1)
                            pe.wait_ge(S["h_done"], (i * 2 + s) * 2 + q + 1)
                            for t in range(4):
                                n = q * 4 + t
                                if n < 4:
                                    pe.wait_ge(S["o_used"], (i * 2 + s) * TT + (n + 1) - 1)
                                else:
                                    pe.wait_ge(S["o_used"], (i * 2 + s) * TT + n - 3)
                                mm(PS[:, 4 + t, 0:D], HH[:, q, t * P:(t + 1) * P], W2,
                                   start=True, stop=True).then_inc(S["o_done"], 1)

            pe.wait_ge(S["flag_ready"], 1)
            with pe.If(pe.value_load(FLAG[0:1, 0:1])):
                all_tokens()
            pe.wait_ge(S["loaded_l1"], 16 * 8)
            pe.wait_ge(S["oe_copied"], E0)
            pe.wait_ge(S["pool_set"], 5)
            pe.wait_ge(S["general_done"], 1)

            def spread(dst, part, which):
                for g in range(UNITS):
                    for i in range(2):
                        last = mm(dst[:, g, :], SPREAD[:, which + i, g % (UNITS // KC), :], part[:, i, g // (UNITS // KC), :],
                                  start=(i == 0), stop=(i == 1))
                return last

            def keys(b):
                pe.wait_ge(S["e_ctx"], b + 1)
                for m in range(KC):
                    last = mm(psKc[:, m, :], WK1[:, m, :], CTB[:, :], start=True, stop=True)
                last.then_inc(S["e_k"], 1)

            def spread_keys(b):
                pe.wait_ge(S["e_spread"], 1)
                pe.wait_ge(S["e_lo_k"], b + 1)
                spread(psK, KP, 0).then_inc(S["e_k_spread"], 1)

            def values(b):
                for t in range(BT):
                    last = mm(psV[:, t, :], CTB[:, t * P:(t + 1) * P], WV1[:, :], start=True, stop=True)
                last.then_inc(S["e_v"], 1)

            def down(f, c):
                pe.wait_ge(S["e_h"], f * NF + c + 1)
                pe.wait_ge(S["e_acc"], f * NF + c)
                for t in range(BT):
                    last = mm(psW[:, t, :], H1[:, c % 2, t * P:(t + 1) * P], WD1[:, c, :], start=True, stop=True)
                last.then_inc(S["e_down"], 1)

            def chunk(f, c):
                if c == 0:
                    pe.wait_ge(S["e_xl"], f + 1)
                if c >= 2:
                    pe.wait_ge(S["e_h"], f * NF + c - 1)
                for a in range(2):
                    for k in range(KC):
                        dst = psGU[:, c % 2, a, :]
                        mm(dst, WGH[:, c, k, a, :], XH[:, k, :], start=(k == 0), stop=False)
                        mm(dst, WGH[:, c, k, a, :], XL[:, k, :], start=False, stop=False)
                        last = mm(dst, WGL[:, c, k, a, :], XH[:, k, :], start=False, stop=(k == KC - 1))
                last.then_inc(S["e_gu"], 1)
                if c:
                    down(f, c - 1)

            def turn(b, f, ahead):

                def fill(c):
                    if f is not None:
                        chunk(f, c)

                fill(0)
                pe.wait_ge(S["e_xn"], b + 1)
                pe.wait_ge(S["e_va"], b + 1)
                pe.wait_ge(S["e_gmax"], b)
                for k in range(KC):
                    for t in range(BT):
                        last = nc.tensor.transpose(psX2[:, k, t * P:(t + 1) * P], XN[:, t, k * P:(k + 1) * P], ident)
                last.then_inc(S["e_flip"], 1)
                fill(1)
                pe.wait_ge(S["e_xt"], b + 1)
                for m in range(KC):
                    for k in range(KC):
                        last = mm(psQc[:, m, :], WQ1[:, k, m, :], XB[:, k, :], start=(k == 0), stop=(k == KC - 1))
                last.then_inc(S["e_q"], 1)
                fill(2)
                pe.wait_ge(S["e_ks"], b + 1)
                pe.wait_ge(S["e_lo_q"], b + 1)
                spread(psQ, QP, 2).then_inc(S["e_q_spread"], 1)
                fill(3)
                pe.wait_ge(S["e_qs"], b * 4 + 4)
                for u in range(UNITS):
                    if u >= 2:
                        pe.wait_ge(S["e_max"], b * UNITS + u - 1)
                    for j in range(2):
                        for t in range(BT):
                            dst = ps1[:, u % 2, j, t * P:t * P + (t + 1) * P]
                            mm(dst, QS[:, u, j, t * P:(t + 1) * P], KS[:, u, 0:(t + 1) * P], start=True, stop=False)
                            last = mm(dst[:, t * P:(t + 1) * P], identb, mask_qk, start=False, stop=True)
                    last.then_inc(S["e_s1"], 1)
                    if u in (2, 5):
                        fill(4 + u // 3)
                fill(6)
                pe.wait_ge(S["e_nm"], b + 1)
                for t in range(BT):
                    last = nc.tensor.transpose(psM[:, t * P:(t + 1) * P],
                                               NMP[:, t, :, :].rearrange("p a h -> p (a h)").bitcast(F32), ident)
                last.then_inc(S["e_flipmax"], 1)
                fill(7)
                pe.wait_ge(S["e_mt"], b + 1)

                def average(g):
                    pe.wait_ge(S["e_exp"], b * NH + (g + 1) * GH)
                    for c in range(BT):
                        for j in range(GH):
                            last = mm(psO[j * HP:(j + 1) * HP, g, c * P:N], VA[:, c, g * GH + j, :],
                                      PP[:, g % 2 * GH + j, c * N:N + c * P], start=(c == 0), stop=(c == BT - 1))
                    last.then_inc(S["e_av"], 1)

                for h in range(NH):
                    if h >= 3:
                        pe.wait_ge(S["e_exp"], b * NH + h - 2)
                    dst, u, j = ps2[:, h % 3, :], h // 2, h % 2
                    mm(dst[:, 0:N], KS[:, u, 0:P], QS[:, u, j, :], start=True, stop=False)
                    mm(dst[:, 0:N], SEL[:, h, :], MT[:, :], start=False, stop=False)
                    mm(dst[:, 0:P], identb, mask_kq, start=False, stop=True)
                    mm(dst[:, N:N + P], KS[:, u, P:N], QS[:, u, j, P:N], start=True, stop=False)
                    mm(dst[:, N:N + P], SEL[:, h, :], MT[:, P:N], start=False, stop=False)
                    mm(dst[:, N:N + P], identb, mask_kq, start=False, stop=True).then_inc(S["e_s2"], 1)
                    if h >= GH and h % GH == 1:
                        average(h // GH - 1)
                average(HG - 1)
                fill(8)
                pe.wait_ge(S["e_os"], b + 1)
                for t in range(BT):
                    for g in range(HG):
                        last = nc.tensor.transpose(PS[:, t, g * P:(g + 1) * P], OS[:, g, t * P:(t + 1) * P], ident)
                last.then_inc(S["e_ot"], 1)
                fill(9)
                pe.wait_ge(S["e_ont"], (b + 1) * BT)
                for k in range(KC):
                    for t in range(BT):
                        last = nc.tensor.transpose(psNT[:, k, t * P:(t + 1) * P], ONT[:, t, k * P:(k + 1) * P], ident)
                last.then_inc(S["e_nt"], 1)
                if f is not None:
                    down(f, NF - 1)
                pe.wait_ge(S["e_on"], b + 1)
                for t in range(BT):
                    for k in range(KC):
                        last = mm(psY[:, t, :], ON[:, k, t * P:(t + 1) * P], WO1[:, k, :], start=(k == 0), stop=(k == KC - 1))
                last.then_inc(S["e_y"], 1)
                if ahead:
                    keys(b + 1)
                    pe.wait_ge(S["e_x3"], b + 1)
                    values(b + 1)
                    spread_keys(b + 1)
                    pe.wait_ge(S["e_va"], b + 2)
                pe.wait_ge(S["e_xn3"], b + 1)
                for k in range(KC):
                    for t in range(BT):
                        last = nc.tensor.transpose(psX3[:, k, t * P:(t + 1) * P], XN3[:, t, k * P:(k + 1) * P], ident)
                last.then_inc(S["e_flip3"], 1)
                pe.wait_ge(S["e_xt3"], b + 1)
                for t in range(BT):
                    for k in range(KC):
                        last = mm(psG[:, t, :], XB3[:, k * N + t * P:k * N + (t + 1) * P], GATE1[:, k, :], start=(k == 0), stop=(k == KC - 1))
                last.then_inc(S["e_gate"], 1)

            keys(0)
            values(0)
            spread_keys(0)
            pe.wait_ge(S["e_wl"], 1)
            pe.wait_ge(S["e_zeros"], 1)
            turn(0, None, True)
            with pe.Fori(0, B - 2) as f:
                turn(f + 1, f, True)
            turn(B - 1, B - 2, False)
            for c in range(NF):
                chunk(B - 1, c)
            down(B - 1, NF - 1)

        @block.scalar
        def _(act):
            A = nc.scalar
            act.wait_ge(S["loaded_raw"], 16)
            A.activation(SC[:, 0:1], RAW[:, 0:1], ACT.Tanh, scale=0.5).then_inc(S["tanh_done"], 1)
            A.activation(SC[:, 1:5], RAW[:, 1:5], ACT.Tanh).then_inc(S["tanh_done"], 1)

            def scores(b):
                act.wait_ge(S["projected"], b + 1)
                A.copy(QK[:, :, :], psQK).then_inc(S["qk_copied"], 1)
                act.wait_ge(S["scores_done"], b + 1)
                act.wait_ge(S["masked"], b)
                A.mul(SIM[:, :, :], psS, SIM_SCALE).then_inc(S["sim_copied"], 1)
                act.wait_ge(S["sim_copied"], b + 1)
                A.activation(TH[:, :, :], SIM[:, :, :], ACT.Tanh, scale=0.5).then_inc(S["act_mix"], 1)
                act.wait_ge(S["act_mix"], b + 1)
                A.add(TH[:, :, :], TH[:, :, :], 1.0).then_inc(S["th_ready"], 1)

            def route(b):
                act.wait_ge(S["xn_ready"], b + 1)
                A.copy(X1[:, ds(b * BT, BT), :], XW[:, :, :])
                A.copy(XNA[:, ds(b * BT, BT), :], XN[:, :, :]).then_inc(S["xna_ready"], 1)
                act.wait_ge(S["xn_flipped"], b + 1)
                A.copy(XNT[:, :, ds(b * N, N)], psX)
                act.wait_ge(S["logits_done"], b)
                A.copy(XB[:, :, :], psX).then_inc(S["xnt_copied"], 1)
                act.wait_ge(S["max_ready"], b + 1)
                for t in range(BT):
                    last = A.activation(EX[:, t, :], LG[:, t, :], ACT.Exp, bias=SM[:, t, 0:1], accum_out=SM[:, t, 1:2])
                last.then_inc(S["exp_done"], 1)

            scores(0)
            with act.Fori(0, B - 1) as b:
                scores(b + 1)
                route(b)
            route(B - 1)
            A.preload_act_table(ACT.Silu)

            def copy_flipped(turn, place):
                e = turn * RING + place
                act.wait_ge(S["xt_flipped"], e + 1)
                if reused(turn, place, 2):
                    act.wait_ge(S["gue_done"], e - 1)
                A.copy(XTE[:, place % 2, :, :], psXE[place % 2]).then_inc(S["xt_copied"], 1)

            def step(turn, place):
                e = turn * RING + place
                if place + 1 < E0:
                    copy_flipped(turn, place + 1)
                act.wait_ge(S["gue_done"], e + 1)
                if reused(turn, place, 2):
                    act.wait_ge(S["he_done"], e - 1)
                A.activation(SGE[:, place % 2, :], psGE[place % 2][:, 0, :], ACT.Silu).then_inc(S["silue_done"], 1)
                if place >= 2:
                    store_slots(turn, place - 2)

            def store_slots(turn, place):
                e = turn * RING + place
                act.wait_ge(S["oe_copied"], e + 1)
                act.dma_start(ys[ds(e * CAP, CAP), :].rearrange("(p r) d -> p r d", r=2), OE[:, place % 3, :, :])\
                   .then_inc(oe_stored[place % 3], 16)

            copy_flipped(0, 0)
            expert_steps(act, step, range(PEEL), range(PEEL + 60, E0))
            store_slots(0, E0 - 2)
            store_slots(0, E0 - 1)

            def all_tokens():
                with act.Fori(0, E0) as e:
                    for q in range(2):
                        act.wait_ge(S["gu_done"], e * 2 + q + 1)
                        if q == 0:
                            act.wait_ge(S["h_done"], e * 2)
                        A.activation(SG[:, q, :], PS[:, 0, :], ACT.Silu).then_inc(S["silu_done"], 1)

            act.wait_ge(S["flag_ready"], 1)
            with act.If(act.value_load(FLAG[0:1, 0:1])):
                all_tokens()
            act.wait_ge(S["loaded_l1"], 16 * 8)
            act.wait_ge(S["all_stored"], 1)
            act.wait_ge(S["general_done"], 1)
            A.copy(WGH[:, :, :, :, :], WGU1[:, :, :, :, :]).then_inc(S["e_wh"], 1)
            A.copy(SPREAD[:, :, :, :], SPREADB[:, :, :, :]).then_inc(S["e_spread"], 1)
            act.wait_ge(S["e_set"], 1)

            def keys_values(b):
                act.wait_ge(S["e_k"], b + 1)
                A.copy(KP[:, 0, :, :], psKc).then_inc(S["e_hi_k"], 1)
                act.wait_ge(S["e_v"], b + 1)
                A.copy(VA[:, :, :, 0:HD], psV.rearrange("p t (h c) -> p t h c", h=NH)).then_inc(S["e_va"], 1)

            def spread_keys(b):
                act.wait_ge(S["e_k_spread"], b + 1)
                A.copy(KS[:, :, :], psK).then_inc(S["e_ks"], 1)

            def chunk(f, c):
                act.wait_ge(S["e_gu"], f * NF + c + 1)
                if c >= 2:
                    act.wait_ge(S["e_h"], f * NF + c - 1)
                A.activation(SG1[:, c % 2, :], psGU[:, c % 2, 0, :], ACT.Silu).then_inc(S["e_silu"], 1)

            def turn(b, f, ahead):

                def fill(c):
                    if f is not None:
                        chunk(f, c)

                fill(0)
                act.wait_ge(S["e_flip"], b + 1)
                A.copy(XB[:, :, :], psX2).then_inc(S["e_xt"], 1)
                A.copy(XR[:, :, :], X2[:, :, :]).then_inc(S["e_xr"], 1)
                fill(1)
                act.wait_ge(S["e_q"], b + 1)
                A.copy(QP[:, 0, :, :], psQc).then_inc(S["e_hi_q"], 1)
                fill(2)
                act.wait_ge(S["e_q_spread"], b + 1)
                for j in range(2):
                    r, g = slice(j * HS, (j + 1) * HS), slice(0, UNITS // 2)
                    A.copy(QS[r, g, j, :], psQ[r, g, :]).then_inc(S["e_qs"], 1)
                for c in range(3, 7):
                    fill(c)
                act.wait_ge(S["e_flipmax"], b + 1)
                A.copy(MT[0:2 * NH, :], psM).then_inc(S["e_mt"], 1)
                fill(7)
                for h in range(NH):
                    act.wait_ge(S["e_s2"], b * NH + h + 1)
                    if h >= 2 * GH:
                        act.wait_ge(S["e_av"], b * HG + h // GH - 1)
                    A.activation(PP[:, h % (2 * GH), :], ps2[:, h % 3, 0:N + P], ACT.Exp, scale=HEAD_SCALE).then_inc(S["e_exp"], 1)
                act.wait_ge(S["e_av"], (b + 1) * HG)
                A.copy(OS[:, :, :], psO).then_inc(S["e_os"], 1)
                fill(8)
                fill(9)
                act.wait_ge(S["e_nt"], b + 1)
                A.copy(ON[:, :, :], psNT).then_inc(S["e_on"], 1)
                if ahead:
                    keys_values(b + 1)
                    spread_keys(b + 1)
                act.wait_ge(S["e_flip3"], b + 1)
                A.copy(XB3[:, :], PS[:, 4, :]).then_inc(S["e_xt3"], 1)
                act.wait_ge(S["e_xt3"], b + 1)
                A.copy(XH.rearrange("p k n -> p (k n)"), XB3[:, :]).then_inc(S["e_xh"], 1)
                act.wait_ge(S["e_gmax"], b + 1)
                for t in range(BT):
                    A.activation(EG[:, t, 0:E1], G14[:, t, 0:E1], ACT.Exp, bias=GS[:, t, 0:1])
                A.activation(EG[:, :, E1:E1 + 1], GS[:, :, 2:3], ACT.Exp, scale=-1.0)
                for t in range(BT):
                    last = A.activation(EG[:, t, E1 + 1:E1 + 2], TP[:, t, 1:2], ACT.Exp, bias=GS[:, t, 0:1])
                last.then_inc(S["e_gexp"], 1)

            keys_values(0)
            spread_keys(0)
            turn(0, None, True)
            with act.Fori(0, B - 2) as f:
                turn(f + 1, f, True)
            turn(B - 1, B - 2, False)
            for c in range(NF):
                chunk(B - 1, c)

        @block.vector
        def _(dve):
            V = nc.vector
            st = Steps(dve, S["dve_scalar"])
            dve.wait_ge(S["tanh_done"], 2)
            st.done(V.tensor_scalar(SC[:, 5:6], SC[:, 0:1], 1.0, 0.125, ALU.add, ALU.mult))
            st.done(V.tensor_scalar(SC[:, 6:7], SC[:, 0:1], -0.5, 0.5, ALU.mult, ALU.add))
            st.wait()
            st.done(V.tensor_tensor(SC[:, 5:6], SC[:, 5:6], SC[:, 1:2], ALU.mult))
            st.done(V.tensor_tensor(SC[:, 6:7], SC[:, 6:7], SC[:, 1:2], ALU.mult))
            st.wait()
            st.done(V.memset(MA[:, :], 0.0))
            st.wait()
            st.end()
            c_graph, c_norm = SC[:, 5:6], SC[:, 6:7]
            c_ffn0, c_att1, c_ffn1 = SC[:, 3:4], SC[:, 2:3], SC[:, 4:5]

            def norm_stats(st, src, ST, MV, RS):
                tiles = ST.shape[1]
                for t in range(tiles):
                    st.done(V.bn_stats(ST[:, t, :], src(t)))
                st.wait()
                for t in range(tiles):
                    st.done(V.bn_aggr(MV[:, t, :], ST[:, t, :]))
                st.wait()
                v, y, h = RS[:, :, 3:4], RS[:, :, 0:1], RS[:, :, 4:5]
                st.done(V.tensor_scalar(v, MV[:, :, 1:2], EPS, None, ALU.add))
                st.wait()
                st.done(V.tensor_scalar(y.bitcast(I32), v.bitcast(I32), -0.5, RSQRT_GUESS, ALU.mult, ALU.add))
                for _ in range(NEWTON):
                    st.wait()
                    st.done(V.scalar_tensor_tensor(h, y, -0.5, y, ALU.mult, ALU.mult))
                    st.wait()
                    st.done(V.tensor_tensor(h, h, v, ALU.mult))
                    st.wait()
                    st.done(V.scalar_tensor_tensor(y, h, 1.5, y, ALU.add, ALU.mult))
                st.wait()

            def norm(st, src, dst):
                norm_stats(st, lambda t: src[:, t, :], ST, MV, RS)
                for t in range(BT):
                    last = V.tensor_scalar(dst[:, t, :], src[:, t, :], MV[:, t, 0:1], RS[:, t, 0:1], ALU.subtract, ALU.mult)
                return last

            dve.wait_ge(S["loaded_x"], 16)
            st = Steps(dve, S["dve_mix"])
            norm_stats(st, lambda t: X[:, t, :], STX, MVX, RSX)
            st.done(V.tensor_scalar(RSX[:, :, 1:2], RSX[:, :, 0:1], c_norm, None, ALU.mult))
            st.wait()
            st.done(V.scalar_tensor_tensor(RSX[:, :, 2:3], MVX[:, :, 0:1], -1.0, RSX[:, :, 1:2], ALU.mult, ALU.mult))
            st.wait()
            st.done(V.tensor_scalar(RSX[:, :, 1:2], RSX[:, :, 1:2], 1.0, None, ALU.add))
            st.wait()

            def threshold(b):
                dve.wait_ge(S["sim_copied"], b + 1)
                for t in range(BT):
                    st.done(V.tensor_scalar(BASE[:, t, :], X[:, ds(b * BT + t, 1), :], RSX[:, ds(b * BT + t, 1), 1:2],
                                            RSX[:, ds(b * BT + t, 1), 2:3], ALU.mult, ALU.add))
                for r in range(ROUNDS):
                    src = SIM if r == 0 else WORK
                    for t in range(BT):
                        if r:
                            st.wait(1)
                        st.done(V.max(TOP[:, t, :], src[:, t, :]))
                    if r < ROUNDS - 1:
                        for t in range(BT):
                            st.wait(1)
                            st.done(V.match_replace(WORK[:, t, :], TOP[:, t, :], src[:, t, :], LOWEST))
                st.wait()

            def mix(b):
                k = (KTH - 1) % 8
                dve.wait_ge(S["th_ready"], b + 1)
                for t in range(BT):
                    last = V.scalar_tensor_tensor(AM[:, t, :], SIM[:, t, :], TOP[:, t, k:k + 1], TH[:, t, :], ALU.is_ge, ALU.mult)
                last.then_inc(S["masked"], 1)
                dve.wait_ge(S["masked"], b + 1)
                st.done(V.scalar_tensor_tensor(XW[:, :, :], AM[:, :, :], c_graph, BASE[:, :, :], ALU.mult, ALU.add))
                st.wait()
                dve.wait_ge(S["flipped"], b + 1)
                st.done(V.scalar_tensor_tensor(XW[:, :, :], psT, c_graph, XW[:, :, :], ALU.mult, ALU.add))
                st.wait()
                norm(st, XW, XN).then_inc(S["xn_ready"], 1)

            def route(b):
                dve.wait_ge(S["logits_done"], b + 1)
                st.done(V.tensor_copy(LG[:, :, :], psL))
                st.wait()
                for t in range(BT):
                    st.done(V.max(L8[:, t, :], LG[:, t, :]))
                st.wait()
                V.tensor_scalar(SM[:, :, 0:1], L8[:, :, 0:1], -1.0, None, ALU.mult).then_inc(S["max_ready"], 1)
                for t in range(BT):
                    st.done(V.match_replace(LR[:, t, :], L8[:, t, :], LG[:, t, :], LOWEST))
                st.wait()
                V.tensor_tensor(MB[:, :, :], LG[:, :, :], LR[:, :, :], ALU.not_equal).then_inc(S["mask_ready"], 1)
                dve.wait_ge(S["mask_ready"], b + 1)
                dve.wait_ge(S["exp_done"], b + 1)
                st.done(V.reciprocal(SM[:, :, 2:3], SM[:, :, 1:2]))
                st.wait()
                for t in range(BT):
                    st.done(V.scalar_tensor_tensor(C0[:, ds(b * BT + t, 1), :], EX[:, t, :], SM[:, t, 2:3], MB[:, t, :], ALU.mult, ALU.mult))
                dve.wait_ge(S["ranked"], b + 1)
                st.done(V.tensor_scalar(OV[:, :, :], psR, float(CAP), None, ALU.is_ge))
                st.done(V.tensor_tensor(K1[:, :, :], psR, slot_base, ALU.add))
                st.done(V.tensor_tensor(MA[:, :], MA[:, :], MB[:, 0, :], ALU.add))
                st.wait()
                st.done(V.tensor_tensor(MA[:, :], MA[:, :], MB[:, 1, :], ALU.add))
                st.done(V.scalar_tensor_tensor(K1[:, :, :], OV[:, :, :], SKIP, K1[:, :, :], ALU.mult, ALU.add))
                st.done(V.tensor_tensor(C0X[:, ds(b * BT, BT), :], C0[:, ds(b * BT, BT), :], OV[:, :, :], ALU.mult))
                st.wait()
                st.done(V.tensor_tensor(K1[:, :, :], K1[:, :, :], MB[:, :, :], ALU.mult))
                st.done(V.tensor_tensor(C0M[:, ds(b * BT, BT), :], C0[:, ds(b * BT, BT), :], C0X[:, ds(b * BT, BT), :], ALU.subtract))
                st.wait()
                for t in range(BT):
                    st.done(V.max(KW[:, t, :], K1[:, t, :]))
                st.done(V.tensor_copy(KEY[:, ds(b * BT, BT), :], K1[:, :, :]))
                st.wait()
                st.done(V.tensor_copy(K8[:, ds(b * BT, BT), :], KW[:, :, :]))
                V.tensor_scalar(IDX[:, ds(b * BT, BT), :], KW[:, :, :], -1.0, None, ALU.add).then_inc(S["idx_ready"], 1)
                st.wait()

            threshold(0)
            st.end()
            with dve.Fori(0, B - 1) as b:
                mix(b)
                threshold(b + 1)
                route(b)
                st.end()
            mix(B - 1)
            route(B - 1)
            st.end()
            st = Steps(dve, S["dve_w8"])
            dve.wait_ge(S["counted"], 1)
            st.done(V.tensor_reduce(FM[:, :], psN, AX.X, ALU.max))
            st.wait()
            V.tensor_scalar(FLAG[:, :], FM[:, :], float(CAP), None, ALU.is_gt).then_inc(S["flag_ready"], 1)
            for t in range(TT):
                st.wait()
                st.done(V.tensor_tensor(EQ[:, :, :], KEY[:, t:t + 1, :].to_broadcast([P, TOP0, E0]),
                                        K8[:, t, :].unsqueeze(2).to_broadcast([P, TOP0, E0]), ALU.is_equal))
                st.wait()
                st.done(V.tensor_tensor(EQ[:, :, :], EQ[:, :, :], C0M[:, t:t + 1, :].to_broadcast([P, TOP0, E0]), ALU.mult))
                st.wait()
                st.done(V.tensor_reduce(W8[:, t, :], EQ[:, :, :], AX.X, ALU.add))
            st.end()

            def copy_out(turn, place):
                e = turn * RING + place
                dve.wait_ge(S["oe_done"], e + 1)
                if reused(turn, place, 3):
                    dve.wait_ge(oe_stored[place % 3], uses(turn, place, 3) * 16)
                V.tensor_copy(OE[:, place % 3, :, :], psOE[place % 2]).then_inc(S["oe_copied"], 1)

            def step(turn, place):
                e = turn * RING + place
                dve.wait_ge(S["silue_done"], e + 1)
                if reused(turn, place, 2):
                    dve.wait_ge(S["oe_done"], e - 1)
                V.tensor_tensor(HE[:, place % 2, :], SGE[:, place % 2, :], psGE[place % 2][:, 1, :], ALU.mult).then_inc(S["he_done"], 1)
                if place:
                    copy_out(turn, place - 1)

            expert_steps(dve, step, range(PEEL), range(PEEL + 60, E0))
            copy_out(0, E0 - 1)

            def all_tokens():
                dve.wait_ge(S["pool_set"], 5)
                with dve.Fori(0, E0) as e:
                    for q in range(2):
                        dve.wait_ge(S["silu_done"], e * 2 + q + 1)
                        if q == 0:
                            dve.wait_ge(S["o_done"], e * TT)
                        V.tensor_tensor(HH[:, q, :], SG[:, q, :], PS[:, 1, :], ALU.mult).then_inc(S["h_done"], 1)
                        for t in range(4):
                            n = q * 4 + t
                            dve.wait_ge(S["o_done"], e * TT + n + 1)
                            V.scalar_tensor_tensor(MOE[:, n, :], PS[:, 4 + t, 0:D], C0X[:, n, ds(e, 1)], MOE[:, n, :],
                                                   ALU.mult, ALU.add).then_inc(S["o_used"], 1)

                dve.wait_ge(S["o_used"], E0 * TT)

            with dve.If(dve.value_load(FLAG[0:1, 0:1])):
                all_tokens()
            dve.sem_inc(S["general_done"], 1)
            dve.wait_ge(S["pool_set"], 5)
            st = Steps(dve, S["dve_l1"])
            dve.wait_ge(S["all_stored"], 1)
            st.done(V.memset(ZP[:, :], 0.0))
            st.wait()
            st.done(V.tensor_copy(MT[:, :], ZP[:, 0:1].to_broadcast([P, N])))
            st.done(V.tensor_copy(SEL[:, :, :], sel_head.unsqueeze(2).to_broadcast([P, NH, P])))
            st.end()
            dve.sem_inc(S["e_set"], 1)
            dve.wait_ge(S["e_wh"], 1)
            V.tensor_tensor(WGL[:, :, :, :, :].rearrange("p c k a n -> p (c k a n)"), WGU1[:, :, :, :, :].rearrange("p c k a n -> p (c k a n)"),
                            WGH[:, :, :, :, :].rearrange("p c k a n -> p (c k a n)").bitcast(F32), ALU.subtract).then_inc(S["e_wl"], 1)
            dve.wait_ge(S["e_wl"], 1)
            V.tensor_copy(QS.rearrange("p g j n -> p (g j n)"), ZP[:, 0:1].to_broadcast([P, UNITS * 2 * N])).then_inc(S["e_zeros"], 1)
            dve.wait_ge(S["e_zeros"], 1)

            def combine(st, b, t):
                dve.wait_ge(gathered[t], (b + 1) * (16 * TOP0))
                for j in range(TOP0):
                    if j:
                        st.wait()
                    so_far = X2[:, t, :] if j else MOE[:, ds(b * BT + t, 1), :]
                    ins = V.scalar_tensor_tensor(X2[:, t, :], GB[:, t, j, :], W8[:, ds(b * BT + t, 1), j:j + 1], so_far, ALU.mult, ALU.add)
                    if j < TOP0 - 1:
                        st.done(ins)
                    else:
                        ins.then_inc(S["gb_used"], 1)

            def enter(st, b):
                dve.wait_ge(S["gb_used"], b * BT + BT)
                st.done(V.scalar_tensor_tensor(X2[:, :, :], X2[:, :, :], c_ffn0, X1[:, ds(b * BT, BT), :], ALU.mult, ALU.add))
                st.wait()
                norm(st, X2, XN).then_inc(S["e_xn"], 1)


            def split_keys(b):
                dve.wait_ge(S["e_hi_k"], b + 1)
                V.tensor_tensor(KP[:, 1, :, :], psKc, KP[:, 0, :, :].bitcast(F32), ALU.subtract).then_inc(S["e_lo_k"], 1)

            def add_up(f, c):
                dve.wait_ge(S["e_down"], f * NF + c + 1)
                dve.wait_ge(S["e_acc"], f * NF + c)
                for t in range(BT):
                    w = CM[:, t, min(c, E1):min(c, E1) + 1]
                    if c == 0:
                        last = V.tensor_scalar(FA[:, t, :], psW[:, t, :], w, None, ALU.mult)
                    else:
                        last = V.scalar_tensor_tensor(FA[:, t, :], psW[:, t, :], w, FA[:, t, :], ALU.mult, ALU.add)
                last.then_inc(S["e_acc"], 1)

            def chunk(f, c):
                dve.wait_ge(S["e_silu"], f * NF + c + 1)
                if c >= 2:
                    dve.wait_ge(S["e_down"], f * NF + c - 1)
                V.tensor_tensor(H1[:, c % 2, :], SG1[:, c % 2, :], psGU[:, c % 2, 1, :], ALU.mult).then_inc(S["e_h"], 1)
                if c:
                    add_up(f, c - 1)

            def leave(f):
                add_up(f, NF - 1)
                dve.wait_ge(S["e_acc"], (f + 1) * NF)
                dve.wait_ge(S["stored"], f * 16)
                V.scalar_tensor_tensor(OUT[:, :, :], FA[:, :, :], c_ffn1, X3[:, :, :], ALU.mult, ALU.add).then_inc(S["e_out"], 1)

            def gates(st, b):
                dve.wait_ge(S["e_gate"], b + 1)
                st.done(V.tensor_copy(G14[:, :, 0:E1], psG[:, :, 0:E1]))
                st.done(V.tensor_copy(GS[:, :, 2:3], psG[:, :, E1:E1 + 1]))
                st.wait()
                for t in range(BT):
                    st.done(V.max(T8[:, t, :], G14[:, t, 0:E1]))
                st.wait()
                st.done(V.tensor_copy(TP[:, :, 0:2], T8[:, :, 0:2]))
                st.done(V.tensor_scalar(GS[:, :, 0:1], T8[:, :, 0:1], -1.0, None, ALU.mult))
                st.wait()
                V.tensor_scalar(GS[:, :, 1:2], T8[:, :, 0:1], 1.0, None, ALU.mult).then_inc(S["e_gmax"], 1)

            def weights(st, b):
                for t in range(BT):
                    st.done(V.match_replace(G14R[:, t, 0:14], TP[:, t, :], G14[:, t, 0:14], LOWEST))
                st.wait()
                st.done(V.tensor_tensor(G14R[:, :, 0:E1], G14[:, :, 0:E1], G14R[:, :, 0:E1], ALU.not_equal))
                dve.wait_ge(S["e_gexp"], b + 1)
                st.done(V.tensor_scalar(EG[:, :, E1:E1 + 2], EG[:, :, E1:E1 + 2], 1.0, None, ALU.add))
                st.wait()
                st.done(V.reciprocal(EG[:, :, E1 + 2:E1 + 4], EG[:, :, E1:E1 + 2]))
                st.wait()
                st.done(V.tensor_copy(CM[:, :, E1:E1 + 1], EG[:, :, E1 + 2:E1 + 3]))
                for t in range(BT):
                    st.done(V.scalar_tensor_tensor(CM[:, t, 0:E1], EG[:, t, 0:E1], EG[:, t, E1 + 3:E1 + 4], G14R[:, t, 0:E1],
                                                   ALU.mult, ALU.mult))
                st.wait()

            def turn(st, b, f, ahead):

                def fill(c):
                    if f is not None:
                        chunk(f, c)

                fill(0)
                if f is not None:
                    weights(st, f)
                fill(1)
                dve.wait_ge(S["e_hi_q"], b + 1)
                V.tensor_tensor(QP[:, 1, :, :], psQc, QP[:, 0, :, :].bitcast(F32), ALU.subtract).then_inc(S["e_lo_q"], 1)
                fill(2)
                dve.wait_ge(S["e_q_spread"], b + 1)
                for j in range(2):
                    r, g = slice(j * HS, (j + 1) * HS), slice(UNITS // 2, UNITS)
                    V.tensor_copy(QS[r, g, j, :], psQ[r, g, :]).then_inc(S["e_qs"], 1)
                fill(3)
                for u in range(UNITS):
                    dve.wait_ge(S["e_s1"], b * UNITS + u + 1)
                    for t in range(BT):
                        last = V.tensor_reduce(NM[:, t, u * 2:(u + 1) * 2], ps1[:, u % 2, :, t * P:t * P + (t + 1) * P],
                                               AX.X, ALU.max, negate=True)
                    last.then_inc(S["e_max"], 1)
                    if u in (2, 5):
                        fill(4 + u // 3)
                dve.wait_ge(S["e_max"], (b + 1) * UNITS)
                st.done(V.tensor_copy(NMP[:, :, 0, :], NM[:, :, :]))
                st.wait()
                V.tensor_tensor(NMP[:, :, 1, :], NM[:, :, :], NMP[:, :, 0, :].bitcast(F32), ALU.subtract).then_inc(S["e_nm"], 1)
                fill(6)
                fill(7)
                if ahead:
                    dve.wait_ge(S["e_xr"], b + 1)
                    for t in range(BT):
                        combine(st, b + 1, t)
                    enter(st, b + 1)
                fill(8)
                dve.wait_ge(S["e_ot"], b + 1)
                st.done(V.reciprocal(RD[:, :, :], psOT[:, :, :, HD]))
                st.wait()
                for t in range(BT):
                    V.tensor_tensor(ONT[:, t, :].rearrange("p (h c) -> p h c", h=NH), psOT[:, t, :, 0:HD],
                                    RD[:, t, :].unsqueeze(2).to_broadcast([P, NH, HD]), ALU.mult).then_inc(S["e_ont"], 1)
                fill(9)
                if f is not None:
                    leave(f)
                    dve.wait_ge(S["e_out"], f + 1)
                dve.wait_ge(S["e_y"], b + 1)
                V.scalar_tensor_tensor(X3[:, :, :], psY, c_att1, XR[:, :, :], ALU.mult, ALU.add).then_inc(S["e_x3"], 1)
                if ahead:
                    split_keys(b + 1)
                dve.wait_ge(S["e_x3"], b + 1)
                norm(st, X3, XN3).then_inc(S["e_xn3"], 1)
                dve.wait_ge(S["e_xh"], b + 1)
                V.tensor_tensor(XL.rearrange("p k n -> p (k n)"), XB3[:, :], XH.rearrange("p k n -> p (k n)").bitcast(F32),
                                ALU.subtract).then_inc(S["e_xl"], 1)
                gates(st, b)

            for t in range(BT):
                combine(st, 0, t)
            enter(st, 0)
            split_keys(0)
            turn(st, 0, None, True)
            st.end()
            with dve.Fori(0, B - 2) as f:
                turn(st, f + 1, f, True)
                st.end()
            turn(st, B - 1, B - 2, False)
            chunk(B - 1, 0)
            weights(st, B - 1)
            for c in range(1, NF):
                chunk(B - 1, c)
            leave(B - 1)
            st.end()


def kernel(**inputs):
    import ml_dtypes
    import numpy as np
    import concourse.bacc as bacc
    from concourse.bass_utils import run_bass_kernel_spmd

    def at(name):
        return np.asarray(inputs[name])

    def chunks(w):
        return w.reshape(-1, P, w.shape[-1]).transpose(1, 0, 2)

    w13, w2 = at("L0_ffn_w13"), at("L0_ffn_w2")
    w13T = w13.transpose(0, 2, 1).reshape(E0, KC, P, 2 * I0).transpose(0, 2, 1, 3).reshape(E0, P, KC * 2 * I0)
    wexp = np.concatenate([w13T, w2.transpose(0, 2, 1)], axis=2).reshape(E0 * P, 3 * D)
    wkv = at("L1_xattn_Wkv_expand").T
    gate = np.concatenate([at("L1_ffn_w_gate"), at("L1_ffn_sh_gate").reshape(2, P, D)])
    up = np.concatenate([at("L1_ffn_w_up"), at("L1_ffn_sh_up").reshape(2, P, D)])
    gu = np.stack([gate, up], axis=1)
    wgu = gu.reshape(NF, 2, P, KC, P).transpose(4, 0, 3, 1, 2)
    down = np.concatenate([at("L1_ffn_w_down").transpose(0, 2, 1), at("L1_ffn_sh_down").T.reshape(2, P, D)])
    raw = np.concatenate([at("L0_xattn_gamma_raw").reshape(1), at("g_xattn"), at("g_ffn")])[None, :]

    row, col = np.arange(P)[:, None], np.arange(P)[None, :]
    cf = np.zeros((P, P + NH + BT * E0), np.float32)
    cf[:, 0:P] = np.eye(P)
    cf[:, P:P + NH] = (row == col[:, :NH]) | (row == NH + col[:, :NH])
    cf[:, P + NH:] = np.tile(np.arange(E0) * CAP + 1, BT)
    spread = np.zeros((P, 4, UNITS // KC, P), ml_dtypes.bfloat16)
    for i, rows in enumerate(((0, 2), (1,), (0, 1), (2,))):
        for g in range(UNITS // KC):
            for j in range(2):
                for r in rows:
                    for d in range(HD):
                        spread[(g * 2 + j) * HD + d, i, g, j * HS + r * HD + d] = 1.0
    cb = np.zeros((P, 5, P), ml_dtypes.bfloat16)
    cb[:, 0] = np.eye(P)
    cb[:, 1] = np.where(col > row, -1.0e38, 0.0)
    cb[:, 2] = np.where(row > col, -1.0e38, 0.0)
    cb[:, 3] = row < col
    cb[:, 4] = 1.0

    ins = {
        "x": at("x").reshape(T, D),
        "ctxT": at("ctx_512").reshape(T, DC).T,
        "raw": raw,
        "wqk0": np.pad(np.stack([at("L0_xattn_Wq").T, at("L0_xattn_Wk").T], axis=1), ((0, 0), (0, 0), (0, P - DC))),
        "gate0": chunks(at("L0_ffn_gate_w").T),
        "wexp": wexp,
        "wq1": chunks(at("L1_xattn_Wq").T).reshape(P, KC, KC, P),
        "wk1": wkv[:, :D].reshape(DC, KC, P),
        "wv1": wkv[:, D:],
        "wo1": chunks(at("L1_xattn_Wout").T),
        "gate1": chunks(np.concatenate([at("L1_ffn_gate_w"), at("L1_ffn_se_gate_w")]).T),
        "wgu1": wgu,
        "wd1": down.transpose(1, 0, 2),
        "spread": spread,
        "cf": cf,
        "cb": cb,
    }
    nc = bacc.Bacc("TRN2", target_bir_lowering=False, num_devices=1)
    arrays, args = {}, []
    for name, a in ins.items():
        a = np.ascontiguousarray(a)
        arrays[f"in_{name}"] = a
        args.append(nc.dram_tensor(f"in_{name}", a.shape, mybir.dt.from_np(a.dtype), kind="ExternalInput").ap())
    args.append(nc.dram_tensor("out_0", (T, D), F32, kind="ExternalOutput").ap())
    xs = nc.dram_tensor("slots_in", (SLOTS, D), F32, kind="Internal").ap()
    ys = nc.dram_tensor("slots_out", (SLOTS, D), F32, kind="Internal").ap()
    gated_block(nc, xs, ys, *args)
    r = run_bass_kernel_spmd(nc, [arrays], core_ids=[0])
    return r.results[0]["out_0"].reshape(B, N, D)
```
